# Optimizing a Trainium2 kernel written in Bass

```python
import numpy as np
import jax
import jax.numpy as jnp

def _softmax(x, axis=-1):
    return jax.nn.softmax(x, axis=axis)

def _gelu(x):
    return jax.nn.gelu(x, approximate=True)

def _silu(x):
    return jax.nn.silu(x)

def _sigmoid(x):
    return jax.nn.sigmoid(x)

def _layernorm(x, axis=-1, eps=1e-05):
    m = jnp.mean(x, axis=axis, keepdims=True)
    v = jnp.var(x, axis=axis, keepdims=True)
    return (x - m) / jnp.sqrt(v + eps)

def _scatter_add(tgt, idx, src, axis=0):
    return tgt.at[idx].add(src)

def _segment_sum(src, seg, n):
    return jax.ops.segment_sum(src, seg, n)
kernel_name = 'mk_prb_d1_jaxref_r8_14e9fd'

def setup_inputs(seed: int=0):
    np.random.seed(seed)
    _w = jnp.asarray

    def _L0_attn_setup():
        import jax, jax.numpy as jnp
        import numpy as np
        B, T = (4, 256)
        D_MODEL = 128
        N_HEADS = 8
        HEAD_DIM = 32
        KV_LRANK = 64

        def _orthogonalize_per_head(w):
            chunks = w.reshape(N_HEADS, HEAD_DIM, D_MODEL)

            def ns(m):
                A = m @ m.T
                Bm = 1.5 * jnp.eye(HEAD_DIM, dtype=m.dtype) - 0.5 * A
                return Bm @ m
            return jax.vmap(ns)(chunks).reshape(w.shape)
        key = jax.random.key(seed)
        ks = jax.random.split(key, 6)

        def lin(k, out_dim, in_dim):
            bound = 1.0 / np.sqrt(in_dim)
            return jax.random.uniform(k, (out_dim, in_dim), jnp.float32, -bound, bound)
        Wq = _orthogonalize_per_head(lin(ks[0], N_HEADS * HEAD_DIM, D_MODEL))
        return {'x': jax.random.normal(ks[1], (B, T, D_MODEL), jnp.float32), 'Wq': Wq, 'Wkv_down': lin(ks[2], KV_LRANK, D_MODEL), 'Wk_up': lin(ks[3], N_HEADS * HEAD_DIM, KV_LRANK), 'Wv_up': lin(ks[4], N_HEADS * HEAD_DIM, KV_LRANK), 'Wo': lin(ks[5], D_MODEL, N_HEADS * HEAD_DIM)}
    _L0_attn_in = _L0_attn_setup()

    def _L0_ffn_setup():
        import jax, jax.numpy as jnp
        import numpy as np
        TOP_K = 2
        key = jax.random.key(seed)
        ks = jax.random.split(key, 5)
        B, T, D, F, E = (2, 256, 128, 512, 8)
        x = jax.random.normal(ks[0], (B, T, D), dtype=jnp.float32)
        router_w = jax.random.normal(ks[1], (D, E + 1), dtype=jnp.float32) * 0.02
        router_b = jax.random.normal(ks[2], (E + 1,), dtype=jnp.float32) * 0.02
        w1 = jax.random.normal(ks[3], (E, D, F), dtype=jnp.float32) * 0.02
        w2 = jax.random.normal(ks[4], (E, F, D), dtype=jnp.float32) * 0.02
        return {'x': x, 'router_w': router_w, 'router_b': router_b, 'w1': w1, 'w2': w2}
    _L0_ffn_in = _L0_ffn_setup()
    _d = {'L0_attn_x': _L0_attn_in['x'], 'L0_attn_Wq': _L0_attn_in['Wq'], 'L0_attn_Wkv_down': _L0_attn_in['Wkv_down'], 'L0_attn_Wk_up': _L0_attn_in['Wk_up'], 'L0_attn_Wv_up': _L0_attn_in['Wv_up'], 'L0_attn_Wo': _L0_attn_in['Wo'], 'L0_ffn_router_w': _L0_ffn_in['router_w'], 'L0_ffn_router_b': _L0_ffn_in['router_b'], 'L0_ffn_w1': _L0_ffn_in['w1'], 'L0_ffn_w2': _L0_ffn_in['w2']}
    _x0 = _d['L0_attn_x']
    _d['L0_attn_x'] = jax.random.normal(jax.random.fold_in(jax.random.key(seed), 1), (4, 1024, 128), dtype=_x0.dtype)
    del _x0
    return _d

def reference(L0_attn_x, L0_attn_Wq, L0_attn_Wkv_down, L0_attn_Wk_up, L0_attn_Wv_up, L0_attn_Wo, L0_ffn_router_w, L0_ffn_router_b, L0_ffn_w1, L0_ffn_w2):

    def _L0_attn_ref(x, Wq, Wkv_down, Wk_up, Wv_up, Wo):
        import jax, jax.numpy as jnp
        import numpy as np
        B, T = (4, 256)
        D_MODEL = 128
        N_HEADS = 8
        HEAD_DIM = 32
        KV_LRANK = 64

        def _orthogonalize_per_head(w):
            chunks = w.reshape(N_HEADS, HEAD_DIM, D_MODEL)

            def ns(m):
                A = m @ m.T
                Bm = 1.5 * jnp.eye(HEAD_DIM, dtype=m.dtype) - 0.5 * A
                return Bm @ m
            return jax.vmap(ns)(chunks).reshape(w.shape)
        b, t, _ = x.shape
        q = (x @ Wq.T).reshape(b, t, N_HEADS, HEAD_DIM)
        kv_latent = x @ Wkv_down.T
        k = (kv_latent @ Wk_up.T).reshape(b, t, N_HEADS, HEAD_DIM)
        v = (kv_latent @ Wv_up.T).reshape(b, t, N_HEADS, HEAD_DIM)
        scale = HEAD_DIM ** (-0.5)
        scores = jnp.einsum('bqhd,bkhd->bhqk', q, k) * scale
        attn = jax.nn.softmax(scores, axis=-1)
        out = jnp.einsum('bhqk,bkhd->bqhd', attn, v)
        out = out.reshape(b, t, N_HEADS * HEAD_DIM)
        return out @ Wo.T

    def _L0_ffn_ref(x, router_w, router_b, w1, w2):
        import jax, jax.numpy as jnp
        import numpy as np
        TOP_K = 2
        E = w1.shape[0]
        logits = x @ router_w + router_b
        probs = jax.nn.softmax(logits, axis=-1)
        top_v, top_i = jax.lax.top_k(probs, TOP_K)
        gates = jnp.sum(jax.nn.one_hot(top_i, E + 1, dtype=x.dtype) * top_v[..., None], axis=-2)
        h = jax.nn.gelu(jnp.einsum('btd,edf->ebtf', x, w1), approximate=False)
        y = jnp.einsum('ebtf,efd->ebtd', h, w2)
        out = jnp.einsum('bte,ebtd->btd', gates[..., :E], y) + gates[..., E:] * x
        return out
    x = L0_attn_x
    xn = _layernorm(x, axis=-1)
    x = x + _L0_attn_ref(xn, L0_attn_Wq, L0_attn_Wkv_down, L0_attn_Wk_up, L0_attn_Wv_up, L0_attn_Wo) + _L0_ffn_ref(xn, L0_ffn_router_w, L0_ffn_router_b, L0_ffn_w1, L0_ffn_w2)
    return x

_drawn_inputs = setup_inputs


def setup_inputs(seed=0):
    import zlib

    import numpy as np

    out = dict(_drawn_inputs(seed))
    spreads = {}
    factors = {'L0_attn_Wq': 7.567,
     'L0_attn_Wkv_down': 7.632,
     'L0_attn_Wk_up': 7.562,
     'L0_attn_Wv_up': 6.046,
     'L0_attn_Wo': 6.062,
     'L0_ffn_router_b': 36.296,
     'L0_ffn_w1': 45.68,
     'L0_ffn_w2': 41.517,
     'L0_ffn_router_w': 8.0}
    for name, (base, spread) in spreads.items():
        noise = np.random.default_rng([zlib.crc32(name.encode()), seed]).standard_normal(out[name].shape)
        drawn = base * np.exp(spread * noise) if base else spread * noise
        out[name] = jnp.asarray(drawn.astype(out[name].dtype))
    for name, factor in factors.items():
        out[name] = (out[name] * factor).astype(out[name].dtype)
    return out
```

```python
import concourse.bass as bass
from concourse import mybir
from contextlib import ExitStack

B, T, D = 4, 1024, 128
H, HD, R = 8, 32, 64
E, F = 8, 512
N = B * T
W = 512
CH = N // W
TILES = N // 128
G = 4
KC = T // 128
FC = F // 128
E1 = E + 1
EPS = 1e-5
SCALE = HD ** -0.5

fp32 = mybir.dt.float32
f32r = mybir.dt.float32r
ALU = mybir.AluOpType
ACT = mybir.ActivationFunctionType
AX = mybir.AxisListType

MAXES = [("max", u) for u in range(G * 4 * 2)] + [("turn", 0)]


def projections(latent):
    lat = [("latent", j) for j in range(2)] if latent else []
    return lat + [(k, j) for j in range(2) for k in ("q", "k")] + [("v", j) for j in range(2)]


def cut(units, sizes):
    out, at = [], 0
    for s in sizes:
        out.append(units[at:at + s])
        at += s
    assert at == len(units)
    return out


def group_steps(g, last):
    nxt = projections(latent=(g == 1))
    half = len(nxt) // 2
    none = last and g == 1
    first = cut(MAXES, [6, 6, 6, 6, 6, 3]) + ([[], []] if none else [nxt[:half], nxt[half:]])
    second = [[]] * 8 if none else [[]] + cut(MAXES, [6, 6, 6, 6, 6, 3]) + [[]]
    return first + second


PROLOGUE = projections(latent=True) + MAXES
BATCH = [u for g in range(2) for s in group_steps(g, False) for u in s]
AUX_BATCH = len(BATCH)
assert AUX_BATCH % 2 == 0
TURNS = [n for n, u in enumerate(BATCH) if u[0] == "turn"]
LAST_SPLIT = [PROLOGUE.index(("q", 1))] + [n for n, u in enumerate(BATCH) if u == ("q", 1)]


def build(nc, xn_d, xT_d, wqT_d, wdT_d, wkT_d, wvT_d, woT_d, rw_d, rb_d, w1_d, w2_d, out_d):
    gates_d = nc.dram_tensor("gates_d", (E1 * TILES, 128), fp32, kind="Internal").ap()
    ctx = ExitStack()
    with ctx:
        def sb(name, shape, dt=fp32, at=ctx):
            return at.enter_context(nc.sbuf_tensor(name, shape, dt))

        def sem(name):
            return ctx.enter_context(nc.semaphore(name))

        ident = sb("ident", [128, 128])
        ones = sb("ones", [128, HD])
        xhi = sb("xhi", [D, N], f32r)
        xlo = sb("xlo", [D, N], f32r)
        acc = sb("acc", [D, N])
        wq_f = sb("wq_f", [D, H * HD])
        wq_hi = sb("wq_hi", [D, H * HD], f32r)
        wq_lo = sb("wq_lo", [D, H * HD], f32r)
        wd_f = sb("wd_f", [D, R])
        wd_hi = sb("wd_hi", [D, R], f32r)
        wd_lo = sb("wd_lo", [D, R], f32r)
        wk = sb("wk", [R, H * HD])
        wv = sb("wv", [R, H * HD])
        wo = sb("wo", [128, 2, D])

        early = ExitStack()
        x = sb("x", [128, TILES, D], at=early)
        stats = sb("stats", [128, TILES, 6], at=early)
        mv = sb("mv", [128, TILES, 2], at=early)
        rstd = sb("rstd", [128, TILES], at=early)
        xn = sb("xn", [128, 2, 4, D], at=early)
        xTf = sb("xTf", [D, 2, W], at=early)
        rw = sb("rw", [D, E1], at=early)
        rb = sb("rb", [128, 4, E1], at=early)
        prob = sb("prob", [128, TILES, E1], at=early)
        key = sb("key", [128, TILES, E1], at=early)
        pick = sb("pick", [128, TILES, E1], at=early)
        left = sb("left", [128, TILES, E1], at=early)
        rank = sb("rank", [128, TILES, E1], at=early)
        top = sb("top", [128, TILES], at=early)
        gates = sb("gates", [128, E1, TILES], at=early)
        gatesT = sb("gatesT", [3 * TILES, 3, 128], at=early)
        gbc = sb("gbc", [128, 2, N], at=early)
        gid = sb("gid", [128, N], at=early)
        w1_f = sb("w1_f", [D, F], at=early)
        w2_f = sb("w2_f", [128, FC, D], at=early)
        w1_hi = sb("w1_hi", [D, 2, F], f32r, at=early)
        w1_lo = sb("w1_lo", [D, 2, F], f32r, at=early)
        w2_hi = sb("w2_hi", [128, 2, FC, D], f32r, at=early)
        w2_lo = sb("w2_lo", [128, 2, FC, D], f32r, at=early)
        hf = sb("hf", [128, 2, W], at=early)
        h_hi = sb("h_hi", [128, 2, FC, W], f32r, at=early)
        h_lo = sb("h_lo", [128, 2, FC, W], f32r, at=early)
        yg = sb("yg", [D, 2, W], at=early)
        same = sb("same", [D, W], at=early)
        early.close()

        qst = [sb(f"qst{i}", [3 * HD + 1, G, T], f32r) for i in range(2)]
        kst = [sb(f"kst{i}", [3 * HD + 1, G, T], f32r) for i in range(2)]
        q_hi = sb("q_hi", [128, T], f32r)
        q_lo = sb("q_lo", [128, T], f32r)
        k_hi = sb("k_hi", [128, T], f32r)
        k_lo = sb("k_lo", [128, T], f32r)
        lat = sb("lat", [R, T])
        v = [sb(f"v{i}", [128, KC, 128]) for i in range(2)]
        P = [sb(f"P{i}", [128, G, W]) for i in range(4)]
        Psum = sb("Psum", [128, G, W])
        halfmax = sb("halfmax", [128, 2, G * 4, 2])
        qmax = sb("qmax", [128, 2, G * 4])
        maxT = sb("maxT", [G * 4, 2, 128], f32r)
        oT = sb("oT", [128, W])
        rden = sb("rden", [128, W])
        on = sb("on", [128, W])

        ps = [ctx.enter_context(nc.psum_tensor(f"ps{i}", [128, 2, W], fp32)) for i in range(2)]
        aux = [ctx.enter_context(nc.psum_tensor(f"aux{i}", [128, W], fp32)) for i in range(2)]
        ps_o = ctx.enter_context(nc.psum_tensor("ps_o", [128, W], fp32))
        ps_d = ctx.enter_context(nc.psum_tensor("ps_d", [128, W], fp32))

        x_in = [sem(f"x_in{i}") for i in range(4)]
        res_in = sem("res_in")
        const_in = sem("const_in")
        zeroed = sem("zeroed")
        ident_set = sem("ident_set")
        chain = sem("chain")
        var_set = sem("var_set")
        std_set = sem("std_set")
        xn_set = sem("xn_set")
        xn_turned = sem("xn_turned")
        xT_copied = sem("xT_copied")
        xlo_set = sem("xlo_set")
        logits_set = sem("logits_set")
        logits_read = sem("logits_read")
        w_hi_set = sem("w_hi_set")
        rec_done = sem("rec_done")
        shifted = sem("shifted")
        exped = sem("exped")
        gates_set = sem("gates_set")
        gates_turned = sem("gates_turned")
        gatesT_set = sem("gatesT_set")
        gates_out = sem("gates_out")
        gid_in = sem("gid_in")
        w_in = sem("w_in")
        gbc_in = [sem(f"gbc_in{i}") for i in range(2)]
        w_split = sem("w_split")
        up_done = sem("up_done")
        gelu_done = sem("gelu_done")
        hlo_done = sem("hlo_done")
        down_done = sem("down_done")
        yg_done = sem("yg_done")
        yg_added = sem("yg_added")
        same_a = sem("same_a")
        stack_ones = sem("stack_ones")
        aux_ready = sem("aux_ready")
        aux_free = [sem(f"aux_free{i}") for i in range(2)]
        hi_done = sem("hi_done")
        qmax_done = sem("qmax_done")
        stacked = [sem(f"stacked{i}") for i in range(2)]
        max_in = [sem(f"max_in{i}") for i in range(2)]
        st_ready = sem("st_ready")
        exp_done = sem("exp_done")
        pv_done = sem("pv_done")
        psum_done = sem("psum_done")
        den_done = sem("den_done")
        o_copied = sem("o_copied")
        on_done = sem("on_done")
        wo_done = sem("wo_done")
        attn_added = sem("attn_added")
        out_done = sem("out_done")

        PAIRS = E // 2
        ITEMS = 2 * CH
        STACK = 16 * 6 * G
        ROW = 16 * G
        CONSTS = 16 * 10

        def split3(out, w_hi, w_lo, m_hi, m_lo, start, stop):
            nc.tensor.matmul(out, w_hi, m_lo, start=start, stop=False)
            nc.tensor.matmul(out, w_lo, m_hi, start=False, stop=False)
            return nc.tensor.matmul(out, w_hi, m_hi, start=False, stop=stop)

        def sections(eng, batch):
            batch(0, True, False)
            with eng.Fori(1, B - 1) as b:
                batch(b, False, False)
            batch(B - 1, False, True)

        def aux_at(b, local):
            return len(PROLOGUE) + AUX_BATCH * b + local

        def aux_bank(local):
            return (len(PROLOGUE) + local) % 2

        def aux_turn(b, local):
            return (AUX_BATCH // 2) * b + (len(PROLOGUE) + local) // 2

        def wait_unit_read(eng, b, local):
            eng.wait_ge(aux_free[aux_bank(local)], aux_turn(b, local) + 1)

        block = ctx.enter_context(nc.Block())

        @block.sync
        def _(sp):
            xv = xn_d.rearrange("(t p) d -> p t d", p=128)
            for i in range(4):
                sp.dma_start(x[:, 8 * i:8 * i + 8, :], xv[:, 8 * i:8 * i + 8, :]).then_inc(x_in[i], 16)
            sp.dma_start(rw[:, :], rw_d).then_inc(const_in, 16)
            for t in range(4):
                sp.dma_start(rb[:, t, :], rb_d.partition_broadcast(128)).then_inc(const_in, 16)
            sp.dma_start(wq_f[:, :], wqT_d).then_inc(const_in, 16)
            sp.dma_start(wd_f[:, :], wdT_d).then_inc(const_in, 16)
            sp.dma_start(wk[:, :], wkT_d).then_inc(const_in, 16)
            sp.dma_start(wv[:, :], wvT_d).then_inc(const_in, 16)
            sp.dma_start(wo[:, :, :], woT_d.rearrange("(g p) d -> p g d", p=128)).then_inc(const_in, 16)
            sp.dma_start(w1_f[:, :], w1_d[0]).then_inc(w_in, 16)
            sp.dma_start(w2_f[:, :, :], w2_d[0].rearrange("(c p) d -> p c d", p=128)).then_inc(w_in, 16)
            sp.dma_start(acc[:, :], xT_d).then_inc(res_in, 16)
            sp.wait_ge(gatesT_set, 1)
            sp.dma_start(gates_d.rearrange("(a r) t -> r a t", a=3), gatesT[:, :, :]).then_inc(gates_out, 16)
            sp.wait_ge(gates_out, 16)
            rows = gates_d.rearrange("(e t) p -> e (t p)", e=E1)
            for j in range(2):
                sp.dma_start(gbc[:, j, :], rows[j].partition_broadcast(128)).then_inc(gbc_in[j], 16)
            sp.dma_start(gid[:, :], rows[E].partition_broadcast(128)).then_inc(gid_in, 16)

            def load_weights(e):
                sp.wait_ge(w_split, e)
                sp.dma_start(w1_f[:, :], w1_d[bass.ds(e, 1)].rearrange("e d f -> d (e f)")).then_inc(w_in, 16)
                sp.dma_start(w2_f[:, :, :],
                             w2_d[bass.ds(e, 1)].rearrange("e (c p) d -> p (e c) d", p=128)).then_inc(w_in, 16)

            def pair(p, last):
                for j in range(2):
                    if not (last and j == 1):
                        load_weights(2 * p + j + 1)
                if not last:
                    for j in range(2):
                        sp.wait_ge(yg_done, 2 + ITEMS * p + CH * (j + 1))
                        sp.dma_start(gbc[:, j, :], rows[bass.ds(2 * p + j + 2, 1)].rearrange("e n -> (e n)")
                                     .partition_broadcast(128)).then_inc(gbc_in[j], 16)

            with sp.Fori(0, PAIRS - 1) as p:
                pair(p, False)
            pair(PAIRS - 1, True)

            def stack(b, unit, n, par, old):
                for k in range(2):
                    wait_unit_read(sp, b, unit + k)
                if old:
                    sp.wait_ge(st_ready, 32 * n - 32)
                for dst, parts in ((kst[par], (k_hi, k_lo, k_hi)), (qst[par], (q_hi, q_hi, q_lo))):
                    for h in range(G):
                        for r, src in enumerate(parts):
                            sp.dma_start(dst[HD * r:HD * (r + 1), h, :].bitcast(fp32),
                                         src[HD * h:HD * (h + 1), :].bitcast(fp32)).then_inc(stacked[par], 16)

            def max_row(b, unit, k):
                wait_unit_read(sp, b, unit)
                par, half = (k % 4) // 2, k % 2
                for h in range(G):
                    sp.dma_start(qst[par][3 * HD:3 * HD + 1, h, W * half:W * (half + 1)].bitcast(fp32),
                                 maxT[4 * h:4 * h + 4, k % 2, :].bitcast(fp32)).then_inc(max_in[k % 2], 16)

            def store(b):
                for half in range(2):
                    sp.wait_ge(attn_added, 4 * b + 3 + half)
                    at = T * b + W * half
                    sp.dma_start(out_d[:, bass.ds(at, W)], acc[:, bass.ds(at, W)]).then_inc(out_done, 16)

            sp.wait_ge(stack_ones, 2)
            stack(0, LAST_SPLIT[0] - len(PROLOGUE), 0, 0, False)
            max_row(0, -1, 0)

            def batch(b, first, last):
                max_row(b, TURNS[0], 1)
                stack(b, LAST_SPLIT[1], 2 * b + 1, 1, not first)
                max_row(b, TURNS[1], 2)
                if not first:
                    store(b - 1)
                max_row(b, TURNS[2], 3)
                if not last:
                    stack(b, LAST_SPLIT[2], 2 * b + 2, 0, True)
                    max_row(b, TURNS[3], 4)

            sections(sp, batch)
            store(B - 1)
            sp.wait_ge(out_done, 16 * CH)

        @block.gpsimd
        def _(pool):
            nc.gpsimd.memset(ident[:, :], 0.0).then_inc(zeroed, 1)
            nc.gpsimd.memset(ones[:, :], 1.0).then_inc(zeroed, 1)
            nc.gpsimd.iota(rank[:, :, :], pattern=[[0, TILES], [-1, E1]], base=2 * E1, channel_multiplier=0,
                           allow_small_or_imprecise_dtypes=True).then_inc(zeroed, 1)
            pool.wait_ge(zeroed, 3)
            nc.gpsimd.affine_select(out=ident[:, :], in_=ident[:, :], compare_op=ALU.not_equal, fill=1.0, base=0,
                                    pattern=[[-1, 128]], channel_multiplier=1).then_inc(ident_set, 1)
            pool.sem_inc(yg_added, 2)
            pool.wait_ge(res_in, 16)

            def add_gated(m, i):
                pool.wait_ge(yg_done, 3 + m)
                cols = slice(W * i, W * (i + 1))
                nc.gpsimd.tensor_tensor(acc[:, cols], acc[:, cols], yg[:, i % 2, :], ALU.add).then_inc(yg_added, 1)

            with pool.Fori(0, PAIRS - 1) as p:
                for k in range(ITEMS):
                    pool.wait_ge(yg_added, 2 + ITEMS * p + k)
                    add_gated(ITEMS * p + k, k % CH)
            pool.wait_ge(gid_in, 16)
            steps = 0
            for k in range(ITEMS):
                m = ITEMS * (PAIRS - 1) + k
                pool.wait_ge(yg_added, 2 + m)
                add_gated(m, k % CH)
                if k < CH:
                    cols = slice(W * k, W * (k + 1))
                    if steps:
                        pool.wait_ge(same_a, steps)
                    nc.gpsimd.tensor_tensor(same[:, :], xhi[:, cols].bitcast(fp32), xlo[:, cols].bitcast(fp32),
                                            ALU.add).then_inc(same_a, 1)
                    pool.wait_ge(same_a, steps + 1)
                    nc.gpsimd.tensor_tensor(same[:, :], same[:, :], gid[:, cols], ALU.mult).then_inc(same_a, 1)
                    pool.wait_ge(same_a, steps + 2)
                    pool.wait_ge(yg_added, 3 + m)
                    nc.gpsimd.tensor_tensor(acc[:, cols], acc[:, cols], same[:, :], ALU.add).then_inc(same_a, 1)
                    steps += 3
            pool.wait_ge(same_a, steps)
            pool.wait_ge(yg_added, 2 + CH * E)
            for i in range(2):
                nc.gpsimd.memset(kst[i][3 * HD:3 * HD + 1, :, :].bitcast(fp32), 1.0).then_inc(stack_ones, 1)

            def pair_sum(i, k, j):
                J = 4 * i + j
                pool.wait_ge(exp_done, 16 * i + 4 * j + 4)
                if not (k == "first" and j == 0):
                    pool.wait_ge(den_done, J)
                a, c = P[(2 * j) % 4], P[(2 * j + 1) % 4]
                nc.gpsimd.tensor_tensor(Psum[:, :, :], a[:, :, :], c[:, :, :], ALU.add).then_inc(psum_done, 1)

            def batch(b, first, last):
                for k in range(4):
                    for j in range(4):
                        pair_sum(4 * b + k, "first" if first and k == 0 else k, j)

            sections(pool, batch)

        @block.scalar
        def _(act):
            act.sem_inc(gelu_done, 4)
            act.wait_ge(var_set, 1)
            nc.scalar.activation(rstd[:, :], rstd[:, :], ACT.Sqrt).then_inc(std_set, 1)
            with act.Fori(0, CH // 2) as c2:
                for j in range(2):
                    c = 2 * c2 + j
                    act.wait_ge(xn_turned, c + 1)
                    cols = bass.ds(W * c, W)
                    nc.scalar.copy(xTf[:, j, :], aux[j][:, :])
                    nc.scalar.copy(xhi[:, cols], aux[j][:, :]).then_inc(xT_copied, 1)
            act.wait_ge(shifted, 1)
            nc.scalar.activation(prob[:, :, :], prob[:, :, :], ACT.Exp).then_inc(exped, 1)
            act.wait_ge(gates_turned, 1)
            nc.scalar.copy(gatesT[:, :, :],
                           ps_d[0:3 * TILES, 0:384].rearrange("r (a t) -> r a t", a=3)).then_inc(gatesT_set, 1)

            def gelu(p, k):
                m = ITEMS * p + k
                for c in range(FC):
                    u = FC * m + c
                    act.wait_ge(up_done, u + 1)
                    if c == 0:
                        act.wait_ge(down_done, m + 1)
                    act.wait_ge(hlo_done, u + 1)
                    src = ps[c // 2][:, c % 2, :]
                    nc.scalar.activation(h_hi[:, k % 2, c, :], src, ACT.Gelu)
                    nc.scalar.activation(hf[:, c % 2, :], src, ACT.Gelu).then_inc(gelu_done, 1)

            with act.Fori(0, PAIRS) as p:
                for k in range(ITEMS):
                    gelu(p, k)

            def exps(b, first, last):
                local, proj = 0, 0
                for g in range(2):
                    n = 2 * b + g
                    for s, units in enumerate(group_steps(g, last)):
                        i, c = 2 * n + s // 8, s % 8
                        for hp in range(2):
                            u = 16 * i + 2 * c + hp
                            act.wait_ge(st_ready, u + 1)
                            if not (first and g == 0 and s < 4):
                                act.wait_ge(pv_done, 8 * i + c - 3)
                                act.wait_ge(psum_done, 4 * i + c // 2 - 1)
                            nc.scalar.activation(P[c % 4][:, 2 * hp:2 * hp + 2, :], ps[hp][:, :, :], ACT.Exp,
                                                 scale=SCALE).then_inc(exp_done, 1)
                        if c == 0 and not (first and g == 0 and s == 0):
                            copy_o(i - 1, first and g == 0 and s == 8)
                        for kind, j in units:
                            project(b, g + 1, kind, j, aux_at(b, local), aux_bank(local))
                            local += 1

            def copy_o(i, start):
                act.wait_ge(pv_done, 8 * i + 8)
                if not start:
                    act.wait_ge(on_done, i)
                nc.scalar.copy(oT[:, :], ps_o[:, :]).then_inc(o_copied, 1)

            def project(b, g, kind, j, at, bank):
                cols, par = slice(W * j, W * (j + 1)), g % 2
                if kind not in ("q", "k", "latent", "v"):
                    return
                act.wait_ge(aux_ready, at + 1)
                if kind in ("q", "k"):
                    if j == 0 and b is not None:
                        act.wait_ge(stacked[1 - par], STACK * (b + 1))
                    dst = q_hi if kind == "q" else k_hi
                    nc.scalar.copy(dst[:, cols], aux[bank][:, :]).then_inc(hi_done, 1)
                elif kind == "latent":
                    nc.scalar.copy(lat[:, cols], aux[bank][0:R, :]).then_inc(aux_free[bank], 1)
                else:
                    nc.scalar.copy(v[par][:, 4 * j:4 * j + 4, :],
                                   aux[bank][:, :].rearrange("p (t d) -> p t d", t=4)).then_inc(aux_free[bank], 1)

            act.wait_ge(stack_ones, 2)
            for at, (kind, j) in enumerate(PROLOGUE):
                project(None, 0, kind, j, at, at % 2)
            sections(act, exps)
            act.wait_ge(pv_done, 8 * 4 * B)
            act.wait_ge(on_done, 4 * B - 1)
            nc.scalar.copy(oT[:, :], ps_o[:, :]).then_inc(o_copied, 1)

        @block.vector
        def _(dve):
            links = [0]

            def link(ins):
                links[0] += 1
                ins.then_inc(chain, 1)
                dve.wait_ge(chain, links[0])

            dve.sem_inc(hlo_done, 2)
            dve.sem_inc(yg_done, 2)
            for t in range(TILES):
                if t % 8 == 0:
                    dve.wait_ge(x_in[t // 8], 16)
                last = nc.vector.bn_stats(stats[:, t, :], x[:, t, :])
            link(last)
            for t in range(TILES):
                last = nc.vector.bn_aggr(mv[:, t, :], stats[:, t, :])
            link(last)
            nc.vector.tensor_scalar(rstd[:, :], mv[:, :, 1], EPS, None, ALU.add).then_inc(var_set, 1)
            dve.wait_ge(std_set, 1)
            link(nc.vector.reciprocal(rstd[:, :], rstd[:, :]))
            dve.wait_ge(const_in, CONSTS)

            def norm(c, j):
                for q in range(4):
                    t = 4 * c + q
                    last = nc.vector.tensor_scalar(xn[:, j, q, :], x[:, bass.ds(t, 1), :].rearrange("p t d -> p (t d)"),
                                                   mv[:, bass.ds(t, 1), 0], rstd[:, bass.ds(t, 1)],
                                                   ALU.subtract, ALU.mult)
                last.then_inc(xn_set, 1)

            with dve.Fori(0, CH // 2) as c2:
                for j in range(2):
                    norm(2 * c2 + j, j)
                for j in range(2):
                    c = 2 * c2 + j
                    dve.wait_ge(xT_copied, c + 1)
                    cols = bass.ds(W * c, W)
                    nc.vector.tensor_tensor(xlo[:, cols], aux[j][:, :], xhi[:, cols].bitcast(fp32),
                                            ALU.subtract).then_inc(xlo_set, 1)
                    dve.wait_ge(logits_set, c + 1)
                    nc.vector.tensor_tensor(prob[:, bass.ds(4 * c, 4), :],
                                            (ps_o, ps_d)[j][:, 0:4 * E1].rearrange("p (t e) -> p t e", t=4),
                                            rb[:, :, :], ALU.add).then_inc(logits_read, 1)
            dve.wait_ge(logits_read, CH)

            wide = [128, TILES, E1]
            bc = top[:, :].unsqueeze(2).to_broadcast(wide)
            link(nc.vector.reduce_max(top[:, :], prob[:, :, :], AX.X))
            nc.vector.tensor_tensor(prob[:, :, :], prob[:, :, :], bc, ALU.subtract).then_inc(shifted, 1)
            dve.wait_ge(exped, 1)
            link(nc.vector.reduce_sum(top[:, :], prob[:, :, :], AX.X))
            link(nc.vector.reciprocal(top[:, :], top[:, :]))
            link(nc.vector.tensor_tensor(prob[:, :, :], prob[:, :, :], bc, ALU.mult))
            dve.wait_ge(ident_set, 1)

            def choose(src, onehot):
                link(nc.vector.reduce_max(top[:, :], src, AX.X))
                link(nc.vector.tensor_tensor(key[:, :, :], src, bc, ALU.is_equal))
                link(nc.vector.tensor_tensor(key[:, :, :], key[:, :, :], rank[:, :, :], ALU.mult))
                link(nc.vector.reduce_max(top[:, :], key[:, :, :], AX.X))
                link(nc.vector.tensor_tensor(onehot, key[:, :, :], bc, ALU.is_equal))

            choose(prob[:, :, :], pick[:, :, :])
            link(nc.vector.scalar_tensor_tensor(out=left[:, :, :], in0=pick[:, :, :], scalar=-2.0,
                                                in1=prob[:, :, :], op0=ALU.mult, op1=ALU.add))
            choose(left[:, :, :], key[:, :, :])
            link(nc.vector.tensor_tensor(key[:, :, :], key[:, :, :], pick[:, :, :], ALU.add))
            nc.vector.tensor_tensor(gates[:, :, :].rearrange("p e t -> p t e"), prob[:, :, :], key[:, :, :],
                                    ALU.mult).then_inc(gates_set, 1)
            link(nc.vector.tensor_copy(wq_hi[:, :], wq_f[:, :]))
            link(nc.vector.tensor_copy(wd_hi[:, :], wd_f[:, :]))
            link(nc.vector.tensor_tensor(wq_lo[:, :], wq_f[:, :], wq_hi[:, :].bitcast(fp32), ALU.subtract))
            link(nc.vector.tensor_tensor(wd_lo[:, :], wd_f[:, :], wd_hi[:, :].bitcast(fp32), ALU.subtract))

            def split_weights(e, par):
                dve.wait_ge(w_in, 32 * e + 32)
                nc.vector.tensor_copy(w1_hi[:, par, :], w1_f[:, :])
                nc.vector.tensor_copy(w2_hi[:, par, :, :], w2_f[:, :, :]).then_inc(w_hi_set, 1)
                dve.wait_ge(w_hi_set, e + 1)
                nc.vector.tensor_tensor(w1_lo[:, par, :], w1_f[:, :], w1_hi[:, par, :].bitcast(fp32), ALU.subtract)
                nc.vector.tensor_tensor(w2_lo[:, par, :, :], w2_f[:, :, :], w2_hi[:, par, :, :].bitcast(fp32),
                                        ALU.subtract).then_inc(w_split, 1)

            def gate(p, k):
                m = ITEMS * p + k
                dve.wait_ge(down_done, 3 + m)
                dve.wait_ge(yg_added, 1 + m)
                if k % CH == 0:
                    dve.wait_ge(gbc_in[k // CH], 16 * p + 16)
                i = k % CH
                nc.vector.tensor_tensor(yg[:, k % 2, :], aux[k % 2][:, :], gbc[:, k // CH, W * i:W * (i + 1)],
                                        ALU.mult).then_inc(yg_done, 1)

            def pair(p, last):
                for k in range(ITEMS):
                    m = ITEMS * p + k
                    for c in range(FC):
                        dve.wait_ge(gelu_done, 4 + FC * m + c + 1)
                        nc.vector.tensor_tensor(h_lo[:, k % 2, c, :], hf[:, c % 2, :],
                                                h_hi[:, k % 2, c, :].bitcast(fp32), ALU.subtract).then_inc(hlo_done, 1)
                    if k:
                        gate(p, k - 1)
                    if k % CH == 2 and not (last and k > CH):
                        split_weights(2 * p + k // CH + 1, (k // CH + 1) % 2)
                gate(p, ITEMS - 1)

            split_weights(0, 0)
            with dve.Fori(0, PAIRS - 1) as p:
                pair(p, False)
            pair(PAIRS - 1, True)

            def unit(b, g, k, kind, j, at, local):
                bank = aux_bank(local)
                if kind in ("max", "turn"):
                    dve.wait_ge(aux_ready, at + 1)
                if kind == "max":
                    nc.vector.reduce_max(halfmax[:, k % 2, j // 2, j % 2:j % 2 + 1], aux[bank][:, :],
                                         AX.X).then_inc(aux_free[bank], 1)
                    if j == 2 * 4 * G - 1:
                        wait_unit_read(dve, b, local - 1)
                        wait_unit_read(dve, b, local)
                        nc.vector.tensor_tensor(qmax[:, k % 2, :], halfmax[:, k % 2, :, 0], halfmax[:, k % 2, :, 1],
                                                ALU.max).then_inc(qmax_done, 1)
                elif kind == "turn":
                    if not (isinstance(b, int) and b == 0 and k < 2):
                        dve.wait_ge(max_in[k % 2], ROW * (2 * b + k // 2))
                    nc.vector.tensor_scalar(maxT[:, k % 2, :], aux[bank][0:G * 4, 0:128], -1.0, None,
                                            ALU.mult).then_inc(aux_free[bank], 1)
                elif kind in ("q", "k"):
                    hi, lo = (q_hi, q_lo) if kind == "q" else (k_hi, k_lo)
                    dve.wait_ge(hi_done, 4 * (2 * b + g) + 2 * j + (1 if kind == "q" else 2))
                    cols = slice(W * j, W * (j + 1))
                    nc.vector.tensor_tensor(lo[:, cols], aux[bank][:, :], hi[:, cols].bitcast(fp32),
                                            ALU.subtract).then_inc(aux_free[bank], 1)

            def normalise(i):
                dve.wait_ge(den_done, 4 * i + 4)
                nc.vector.reciprocal(rden[:, :], ps_d[:, :]).then_inc(rec_done, 1)
                dve.wait_ge(rec_done, i + 1)
                dve.wait_ge(o_copied, i + 1)
                nc.vector.tensor_tensor(on[:, :], oT[:, :], rden[:, :], ALU.mult).then_inc(on_done, 1)

            def add(i, at):
                dve.wait_ge(wo_done, i + 1)
                cols = bass.ds(at, W)
                nc.vector.tensor_tensor(acc[:, cols], acc[:, cols], ps_d[:, :], ALU.add).then_inc(attn_added, 1)

            def batch(b, first, last):
                local = 0
                for g in range(2):
                    n = 2 * b + g
                    for s, units in enumerate(group_steps(g, last)):
                        i, c, kb = 2 * n + s // 8, s % 8, 2 * g + s // 8
                        for kind, j in units:
                            unit(b, g + 1, kb + 1, kind, j, aux_at(b, local), local)
                            local += 1
                        if first and kb == 0:
                            continue
                        if c == 2:
                            normalise(i - 1)
                        if c == 3:
                            at = T * b + W * ((kb - 1) % 2) if kb else T * b - W
                            add(i - 1, at)

            dve.wait_ge(stack_ones, 2)
            for at, (kind, j) in enumerate(PROLOGUE):
                unit(0, 0, 0, kind, j, at, at - len(PROLOGUE))
            sections(dve, batch)
            normalise(4 * B - 1)
            add(4 * B - 1, N - W)

        @block.tensor
        def _(pe):
            pe.sem_inc(down_done, 2)
            pe.wait_ge(ident_set, 1)
            pe.wait_ge(const_in, CONSTS)
            with pe.Fori(0, CH // 2) as c2:
                for j in range(2):
                    c = 2 * c2 + j
                    pe.wait_ge(xn_set, c + 1)
                    for q in range(4):
                        last = nc.tensor.transpose(aux[j][:, 128 * q:128 * q + 128], xn[:, j, q, :], ident[:, :])
                    last.then_inc(xn_turned, 1)
                    pe.wait_ge(xT_copied, c + 1)
                    for q in range(4):
                        last = nc.tensor.matmul((ps_o, ps_d)[j][:, E1 * q:E1 * (q + 1)], xTf[:, j, 128 * q:128 * q + 128],
                                                rw[:, :], start=True, stop=True)
                    last.then_inc(logits_set, 1)
            pe.wait_ge(gates_set, 1)
            for a in range(3):
                last = nc.tensor.transpose(ps_d[0:3 * TILES, 128 * a:128 * a + 128],
                                           gates[:, 3 * a:3 * a + 3, :].rearrange("p e t -> p (e t)"), ident[:, :])
            last.then_inc(gates_turned, 1)
            pe.wait_ge(xlo_set, CH)

            def up(p, k):
                m, i, par = ITEMS * p + k, k % CH, k // CH
                if i == 0:
                    pe.wait_ge(w_split, 2 * p + par + 1)
                cols = slice(W * i, W * (i + 1))
                for c in range(FC):
                    pe.wait_ge(gelu_done, FC * m + c + 1)
                    w = slice(128 * c, 128 * c + 128)
                    split3(ps[c // 2][:, c % 2, :], w1_hi[:, par, w], w1_lo[:, par, w], xhi[:, cols], xlo[:, cols],
                           True, True).then_inc(up_done, 1)

            def down(p, k):
                m, par = ITEMS * p + k, k // CH
                pe.wait_ge(yg_done, m + 1)
                for c in range(FC):
                    pe.wait_ge(hlo_done, 2 + FC * m + c + 1)
                    last = split3(aux[k % 2][:, :], w2_hi[:, par, c, :], w2_lo[:, par, c, :], h_hi[:, k % 2, c, :],
                                  h_lo[:, k % 2, c, :], c == 0, c == FC - 1)
                last.then_inc(down_done, 1)

            with pe.Fori(0, PAIRS) as p:
                for k in range(ITEMS):
                    up(p, k)
                    if k:
                        down(p, k - 1)
                down(p, ITEMS - 1)

            def unit(b, g, k, kind, j, local, start):
                out, par, b_of = aux[aux_bank(local)], g % 2, b + g // 2
                if not start:
                    wait_unit_read(pe, b, local - 2)
                cols = slice(W * j, W * (j + 1))
                if kind == "max":
                    hh, qt, kh = j // 8, (j // 2) % 4, j % 2
                    gp, half = (k // 2) % 2, k % 2
                    if j == 0:
                        pe.wait_ge(stacked[gp], STACK * (b + k // 4 + 1))
                    q0 = W * half + 128 * qt
                    nc.tensor.matmul(out[:, :], qst[gp][0:3 * HD, hh, q0:q0 + 128],
                                     kst[gp][0:3 * HD, hh, W * kh:W * kh + W], start=True,
                                     stop=True).then_inc(aux_ready, 1)
                elif kind == "turn":
                    pe.wait_ge(qmax_done, 4 * b + k + 1)
                    nc.tensor.transpose(out[0:G * 4, 0:128], qmax[:, k % 2, :], ident[:, :]).then_inc(aux_ready, 1)
                elif kind == "latent":
                    toks = bass.ds(T * b_of + W * j, W)
                    split3(out[0:R, :], wd_hi[:, :], wd_lo[:, :], xhi[:, toks], xlo[:, toks], True,
                           True).then_inc(aux_ready, 1)
                elif kind == "q":
                    toks = bass.ds(T * b_of + W * j, W)
                    w = slice(128 * par, 128 * par + 128)
                    split3(out[:, :], wq_hi[:, w], wq_lo[:, w], xhi[:, toks], xlo[:, toks], True,
                           True).then_inc(aux_ready, 1)
                elif kind == "k":
                    nc.tensor.matmul(out[:, :], wk[:, 128 * par:128 * par + 128], lat[:, cols], start=True,
                                     stop=True).then_inc(aux_ready, 1)
                else:
                    for q in range(4):
                        t = 4 * j + q
                        last = nc.tensor.matmul(out[:, 128 * q:128 * q + 128], lat[:, 128 * t:128 * t + 128],
                                                wv[:, 128 * par:128 * par + 128], start=True, stop=True)
                    last.then_inc(aux_ready, 1)

            def scores(b, i, k, c, hp, start):
                gp, half = k // 2, k % 2
                if not start:
                    pe.wait_ge(exp_done, 16 * i + 2 * c + hp - 1)
                if c == 0 and hp == 0:
                    pe.wait_ge(max_in[k % 2], ROW * (2 * b + k // 2 + 1))
                for x_ in range(2):
                    hh = 2 * hp + x_
                    last = nc.tensor.matmul(ps[hp][:, x_, :], kst[gp][:, hh, 128 * c:128 * c + 128],
                                            qst[gp][:, hh, W * half:W * half + W], start=True, stop=True)
                last.then_inc(st_ready, 1)

            def values(i, k, c, start):
                pe.wait_ge(exp_done, 16 * i + 2 * c + 2)
                gp = k // 2
                if c == 0:
                    if not start:
                        pe.wait_ge(o_copied, i)
                for h in range(G):
                    rows = slice(HD * h, HD * (h + 1))
                    last = nc.tensor.matmul(ps_o[rows, :], v[gp][:, c, rows], P[c % 4][:, h, :], start=(c == 0),
                                            stop=(c == KC - 1), skip_group_check=True)
                last.then_inc(pv_done, 1)

            def denominators(i, j, start):
                pe.wait_ge(psum_done, 4 * i + j + 1)
                if j == 0 and not start:
                    pe.wait_ge(attn_added, i)
                for h in range(G):
                    rows = slice(HD * h, HD * (h + 1))
                    last = nc.tensor.matmul(ps_d[rows, :], ones[:, :], Psum[:, h, :], start=(j == 0), stop=(j == 3),
                                            skip_group_check=True)
                last.then_inc(den_done, 1)

            def output(i, k):
                pe.wait_ge(on_done, i + 1)
                nc.tensor.matmul(ps_d[:, :], wo[:, k // 2, :], on[:, :], start=True, stop=True).then_inc(wo_done, 1)

            def lagging(i, k, c, first):
                k1 = (k - 1) % 4
                if c == 0:
                    if not first:
                        values(i - 1, k1, KC - 1, False)
                else:
                    values(i, k, c - 1, first)
                if c in (4, 6):
                    denominators(i, c // 2 - 2, first)
                if first:
                    return
                if c == 0:
                    denominators(i - 1, 2, False)
                if c == 2:
                    denominators(i - 1, 3, False)
                if c == 3:
                    output(i - 1, k1)

            def batch(b, first, last):
                local = 0
                for g in range(2):
                    n = 2 * b + g
                    for s, units in enumerate(group_steps(g, last)):
                        i, c, k = 2 * n + s // 8, s % 8, 2 * g + s // 8

                        def beside(us):
                            nonlocal local
                            for kind, j in us:
                                unit(b, g + 1, k + 1, kind, j, local, False)
                                local += 1

                        scores(b, i, k, c, 0, first and s == 0 and g == 0)
                        beside(units[:len(units) // 3])
                        scores(b, i, k, c, 1, first and s == 0 and g == 0)
                        beside(units[len(units) // 3:2 * len(units) // 3])
                        lagging(i, k, c, first and k == 0)
                        beside(units[2 * len(units) // 3:])

            for at, (kind, j) in enumerate(PROLOGUE):
                if at < 2:
                    pe.wait_ge(yg_done, 2 + E * CH)
                unit(0, 0, 0, kind, j, at - len(PROLOGUE), at < 2)
            sections(pe, batch)
            i = 4 * B - 1
            values(i, 3, KC - 1, False)
            denominators(i, 2, False)
            denominators(i, 3, False)
            output(i, 3)


def kernel(L0_attn_x, L0_attn_Wq, L0_attn_Wkv_down, L0_attn_Wk_up, L0_attn_Wv_up, L0_attn_Wo, L0_ffn_router_w,
           L0_ffn_router_b, L0_ffn_w1, L0_ffn_w2):
    import numpy as np
    import concourse.bacc as bacc
    from concourse.bass_utils import run_bass_kernel_spmd

    x = np.ascontiguousarray(L0_attn_x).reshape(N, D)
    arrays = {
        "x_dram": x,
        "xT_dram": np.ascontiguousarray(x.T),
        "wqT_dram": np.ascontiguousarray(np.asarray(L0_attn_Wq).T),
        "wdT_dram": np.ascontiguousarray(np.asarray(L0_attn_Wkv_down).T),
        "wkT_dram": np.ascontiguousarray(np.asarray(L0_attn_Wk_up).T),
        "wvT_dram": np.ascontiguousarray(np.asarray(L0_attn_Wv_up).T),
        "woT_dram": np.ascontiguousarray(np.asarray(L0_attn_Wo).T),
        "rw_dram": np.ascontiguousarray(L0_ffn_router_w),
        "rb_dram": np.ascontiguousarray(L0_ffn_router_b),
        "w1_dram": np.ascontiguousarray(L0_ffn_w1),
        "w2_dram": np.ascontiguousarray(L0_ffn_w2),
    }
    nc = bacc.Bacc("TRN2", target_bir_lowering=False, num_devices=1)
    ins = [nc.dram_tensor(k, a.shape, mybir.dt.from_np(a.dtype), kind="ExternalInput").ap()
           for k, a in arrays.items()]
    out = nc.dram_tensor("outT", (D, N), fp32, kind="ExternalOutput").ap()
    build(nc, *ins, out)
    r = run_bass_kernel_spmd(nc, [arrays], core_ids=[0])
    return np.ascontiguousarray(np.asarray(r.results[0]["outT"]).T).reshape(B, T, D)
```

```python
import concourse.bass as bass
from concourse import mybir
from contextlib import ExitStack

B, T, D = 4, 1024, 128
H, HD, R = 8, 32, 64
E, F = 8, 512
N = B * T
W = 512
CH = N // W
TILES = N // 128
G = 4
KC = T // 128
FC = F // 128
E1 = E + 1
EPS = 1e-5
SCALE = HD ** -0.5

fp32 = mybir.dt.float32
f32r = mybir.dt.float32r
ALU = mybir.AluOpType
ACT = mybir.ActivationFunctionType
AX = mybir.AxisListType

AB = 3
MAXES = [("max", u) for u in range(G * 4 * 2)] + [("turn", 0)]


def projections(latent):
    lat = [("latent", j) for j in range(2)] if latent else []
    return lat + [(k, j) for j in range(2) for k in ("q", "k")] + [("v", j) for j in range(2)]


def cut(units, sizes):
    out, at = [], 0
    for s in sizes:
        out.append(units[at:at + s])
        at += s
    assert at == len(units)
    return out


def group_steps(g, last):
    nxt = [] if last and g == 1 else projections(latent=(g == 1))
    one = cut(MAXES, [5, 0, 5, 6, 6, 5, 6, 0])
    one[1], one[2] = nxt[:-2], nxt[-2:] + one[2]
    two = [[] for _ in range(8)] if last and g == 1 else cut(MAXES, [4, 4, 5, 5, 5, 5, 5, 0])
    for steps in (one, two):
        steps[7] = [("out", 0)]
    return one + two


PROLOGUE = projections(latent=True) + MAXES
BESIDE_EXPERTS = cut(list(enumerate(PROLOGUE)), [2, 2, 2, 2, 0, 0, 0, 4, 4, 4, 4, 4, 4, 4, 4, 1])
AUX_BATCH = sum(len(s) for g in range(2) for s in group_steps(g, False))
assert AUX_BATCH % AB == 0


def numbered(first, last):
    at = len(PROLOGUE) - (not first)
    for g in range(2):
        for s, units in enumerate(group_steps(g, last)):
            k, out = 2 * g + s // 8, []
            for kind, j in units:
                if not (first and k == 0 and kind == "out"):
                    out.append((kind, j, at))
                    at += 1
            yield g, k, s % 8, out


LAST_OUT = max(no for _, _, _, us in numbered(False, True) for _, _, no in us) + 1


def places(units, n=6):
    return [units[len(units) * j // n:len(units) * (j + 1) // n] for j in range(n)]


def find(first, last, kind, j, k):
    return next(no for _, kk, _, us in numbered(first, last) for t, jj, no in us if (t, jj, kk) == (kind, j, k))


def build(nc, xn_d, xT_d, wqT_d, wdT_d, wkT_d, wvT_d, woT_d, rw_d, rb_d, w1_d, w2_d, out_d):
    gates_d = nc.dram_tensor("gates_d", (E1, TILES, 4, 32), fp32, kind="Internal").ap()
    ctx = ExitStack()
    with ctx:
        def sb(name, shape, dt=fp32, at=ctx):
            return at.enter_context(nc.sbuf_tensor(name, shape, dt))

        def sem(name):
            return ctx.enter_context(nc.semaphore(name))

        ident = sb("ident", [128, 128])
        ones = sb("ones", [128, HD])
        xhi = sb("xhi", [D, N], f32r)
        xlo = sb("xlo", [D, N], f32r)
        acc = sb("acc", [D, N])
        wq_f = sb("wq_f", [D, H * HD])
        wq_hi = sb("wq_hi", [D, H * HD], f32r)
        wq_lo = sb("wq_lo", [D, H * HD], f32r)
        wd_f = sb("wd_f", [D, R])
        wd_hi = sb("wd_hi", [D, R], f32r)
        wd_lo = sb("wd_lo", [D, R], f32r)
        wk = sb("wk", [R, H * HD])
        wv = sb("wv", [R, H * HD])
        wo = sb("wo", [128, 2, D])

        def stacks(i):
            return (sb(f"qst{i}", [3 * HD + 1, 2, G, W], f32r), sb(f"kst{i}", [3 * HD + 1, G, T], f32r))

        early = stacks(0)
        lat = sb("lat", [R, T])
        v = [sb(f"v{i}", [128, KC, 128]) for i in range(2)]
        halfmax = sb("halfmax", [128, 2, G * 4, 2])
        qmax = sb("qmax", [128, 2, G * 4])
        maxT = sb("maxT", [G * 4, 2, 128], f32r)

        with ExitStack() as part:
            gid = sb("gid", [128, N], at=part)
        q_hi = sb("q_hi", [128, T], f32r)
        q_lo = sb("q_lo", [128, T], f32r)
        k_hi = sb("k_hi", [128, T], f32r)
        k_lo = sb("k_lo", [128, T], f32r)

        with ExitStack() as part:
            mv = sb("mv", [128, TILES, 2], at=part)
            rstd = sb("rstd", [128, TILES], at=part)
            rw = sb("rw", [D, E1], at=part)
            rb = sb("rb", [128, 4, E1], at=part)
            prob = sb("prob", [128, TILES, E1], at=part)
            key = sb("key", [128, TILES, E1], at=part)
            pick = sb("pick", [128, TILES, E1], at=part)
            left = sb("left", [128, TILES, E1], at=part)
            rank = sb("rank", [128, TILES, E1], at=part)
            top = sb("top", [128, TILES], at=part)
            gates = sb("gates", [128, E1, TILES], at=part)
            gatesT = sb("gatesT", [128, E1, 32], at=part)
            gbc = sb("gbc", [128, 2, N // 2], at=part)
            w1_f = sb("w1_f", [D, F], at=part)
            w2_f = sb("w2_f", [128, FC, D], at=part)
            w1_hi = sb("w1_hi", [D, 2, F], f32r, at=part)
            w1_lo = sb("w1_lo", [D, 2, F], f32r, at=part)
            w2_hi = sb("w2_hi", [128, 2, FC, D], f32r, at=part)
            w2_lo = sb("w2_lo", [128, 2, FC, D], f32r, at=part)
            hf = sb("hf", [128, 2, W], at=part)
            yg = sb("yg", [D, 2, W], at=part)
            same = sb("same", [D, W], at=part)
            with ExitStack() as norm_part:
                x = sb("x", [128, TILES, D], at=norm_part)
                stats = sb("stats", [128, TILES, 6], at=norm_part)
                xTf = sb("xTf", [D, 2, W], at=norm_part)
            h_hi = sb("h_hi", [128, 2, FC, W], f32r, at=part)
            h_lo = sb("h_lo", [128, 2, FC, W], f32r, at=part)

        late = stacks(1)
        qst, kst = (early[0], late[0]), (early[1], late[1])
        P = [sb(f"P{i}", [128, G, W]) for i in range(4)]
        Psum = [sb(f"Psum{i}", [128, G, W]) for i in range(2)]
        oT = sb("oT", [128, W])
        rden = sb("rden", [128, W])
        on = sb("on", [128, W])

        st = [ctx.enter_context(nc.psum_tensor(f"st{i}", [128, W], fp32)) for i in range(3)]
        aux = [ctx.enter_context(nc.psum_tensor(f"aux{i}", [128, W], fp32)) for i in range(AB)]
        ps_o = ctx.enter_context(nc.psum_tensor("ps_o", [128, W], fp32))
        ps_d = ctx.enter_context(nc.psum_tensor("ps_d", [128, W], fp32))
        up_ps = st + [ps_d]

        x_in = [sem(f"x_in{i}") for i in range(4)]
        res_in = sem("res_in")
        const_in = sem("const_in")
        zeroed = sem("zeroed")
        ident_set = sem("ident_set")
        chain = sem("chain")
        var_set = sem("var_set")
        std_set = sem("std_set")
        xn_set = sem("xn_set")
        recip_set = sem("recip_set")
        x_turned = sem("x_turned")
        xT_copied = sem("xT_copied")
        xlo_set = sem("xlo_set")
        logits_set = sem("logits_set")
        logits_read = sem("logits_read")
        w_hi_set = sem("w_hi_set")
        rec_done = sem("rec_done")
        shifted = sem("shifted")
        exped = sem("exped")
        gates_set = sem("gates_set")
        gatesT_set = sem("gatesT_set")
        gates_out = sem("gates_out")
        gid_in = sem("gid_in")
        w_in = sem("w_in")
        gbc_in = [sem(f"gbc_in{i}") for i in range(2)]
        w_split = sem("w_split")
        up_done = sem("up_done")
        gelu_done = sem("gelu_done")
        hlo_done = sem("hlo_done")
        down_done = sem("down_done")
        yg_done = sem("yg_done")
        yg_added = sem("yg_added")
        same_a = sem("same_a")
        stack_ones = sem("stack_ones")
        ones_in = sem("ones_in")
        aux_ready = sem("aux_ready")
        aux_free = [sem(f"aux_free{i}") for i in range(AB)]
        hi_done = sem("hi_done")
        qmax_done = sem("qmax_done")
        stacked = [sem(f"stacked{i}") for i in range(2)]
        max_in = [sem(f"max_in{i}") for i in range(2)]
        st_ready = sem("st_ready")
        exp_done = sem("exp_done")
        pv_done = sem("pv_done")
        psum_done = sem("psum_done")
        den_done = sem("den_done")
        den_copied = sem("den_copied")
        o_copied = sem("o_copied")
        on_done = sem("on_done")
        out_done = sem("out_done")

        PAIRS = E // 2
        ITEMS = 2 * CH
        STACK = 16 * 6 * G
        CONSTS = 16 * 10

        def split3(out, w_hi, w_lo, m_hi, m_lo, start, stop):
            nc.tensor.matmul(out, w_hi, m_lo, start=start, stop=False)
            nc.tensor.matmul(out, w_lo, m_hi, start=False, stop=False)
            return nc.tensor.matmul(out, w_hi, m_hi, start=False, stop=stop)

        def sections(eng, batch):
            batch(0, True, False)
            with eng.Fori(1, B - 1) as b:
                batch(b, False, False)
            batch(B - 1, False, True)

        ST = G * KC

        def units_read(b, no):
            return AUX_BATCH // AB * b + no // AB + 1

        def wait_unit_read(eng, b, no):
            eng.wait_ge(aux_free[no % AB], units_read(b, no))

        block = ctx.enter_context(nc.Block())

        @block.sync
        def _(sp):
            xv = xn_d.rearrange("(t p) d -> p t d", p=128)
            for i in range(4):
                sp.dma_start(x[:, 8 * i:8 * i + 8, :], xv[:, 8 * i:8 * i + 8, :]).then_inc(x_in[i], 16)
            sp.dma_start(rw[:, :], rw_d).then_inc(const_in, 16)
            for t in range(4):
                sp.dma_start(rb[:, t, :], rb_d.partition_broadcast(128)).then_inc(const_in, 16)
            sp.dma_start(wq_f[:, :], wqT_d).then_inc(const_in, 16)
            sp.dma_start(wd_f[:, :], wdT_d).then_inc(const_in, 16)
            sp.dma_start(wk[:, :], wkT_d).then_inc(const_in, 16)
            sp.dma_start(wv[:, :], wvT_d).then_inc(const_in, 16)
            sp.dma_start(wo[:, :, :], woT_d.rearrange("(g p) d -> p g d", p=128)).then_inc(const_in, 16)
            sp.dma_start(w1_f[:, :], w1_d[0]).then_inc(w_in, 16)
            sp.dma_start(w2_f[:, :, :], w2_d[0].rearrange("(c p) d -> p c d", p=128)).then_inc(w_in, 16)
            sp.dma_start(acc[:, :], xT_d).then_inc(res_in, 16)
            sp.wait_ge(gatesT_set, 1)
            for a in range(4):
                sp.dma_start(gates_d[:, :, a, :].rearrange("e t p -> t e p"),
                             gatesT[32 * a:32 * a + 32, :, :]).then_inc(gates_out, 16)
            sp.wait_ge(gates_out, 64)
            rows = gates_d.rearrange("e t a p -> e (t a p)")

            def load_gates(e, half):
                src = rows[bass.ds(e, 1), N // 2 * half:N // 2 * (half + 1)].rearrange("e n -> (e n)")
                sp.dma_start(gbc[:, half, :], src.partition_broadcast(128)).then_inc(gbc_in[half], 16)

            load_gates(0, 0)
            sp.dma_start(gid[:, :], rows[E].partition_broadcast(128)).then_inc(gid_in, 16)
            load_gates(0, 1)

            def load_weights(e):
                sp.wait_ge(w_split, e)
                sp.dma_start(w1_f[:, :], w1_d[bass.ds(e, 1)].rearrange("e d f -> d (e f)")).then_inc(w_in, 16)
                sp.dma_start(w2_f[:, :, :],
                             w2_d[bass.ds(e, 1)].rearrange("e (c p) d -> p (e c) d", p=128)).then_inc(w_in, 16)

            def pair(p, last):
                for j in range(2):
                    e = 2 * p + j
                    if last and j == 1:
                        max_row(0, len(PROLOGUE) - 1, 0)
                        break
                    load_weights(e + 1)
                    for half in range(2):
                        sp.wait_ge(yg_done, 1 + CH * e + CH // 2 * (half + 1))
                        load_gates(e + 1, half)
                        if last and half == 0:
                            stack(0, PROLOGUE.index(("k", 1)), 0)
            def held(value):
                return value if isinstance(value, int) else sp.snap(value)

            def stack(b, no, par):
                wait_unit_read(sp, b, no)
                for h in range(G):
                    rows = slice(HD * h, HD * (h + 1))
                    for r, src in enumerate((k_hi, k_lo, k_hi)):
                        sp.dma_start(kst[par][HD * r:HD * (r + 1), h, :].bitcast(fp32),
                                     src[rows, :].bitcast(fp32)).then_inc(stacked[par], 16)
                    for r, src in enumerate((q_hi, q_hi, q_lo)):
                        sp.dma_start(qst[par][HD * r:HD * (r + 1), :, h, :].bitcast(fp32),
                                     src[rows, :].rearrange("p (a w) -> p a w", a=2)
                                     .bitcast(fp32)).then_inc(stacked[par], 16)

            def max_row(b, no, k):
                wait_unit_read(sp, b, no)
                par, half = (k % 4) // 2, k % 2
                sp.dma_start(qst[par][3 * HD:3 * HD + 1, half, :, :].rearrange("p h w -> p (h w)").bitcast(fp32),
                             maxT[:, k % 2, :].bitcast(fp32)).then_inc(max_in[k % 2], 16)

            def store(b, no, half):
                at = T * b + W * half if half == 0 or no == LAST_OUT else T * b - W
                at, count = held(at), held(units_read(b, no))
                sp.wait_ge(aux_free[no % AB], count)
                sp.dma_start(out_d[:, bass.ds(at, W)], acc[:, bass.ds(at, W)]).then_inc(out_done, 16)

            with sp.Fori(0, PAIRS - 1) as p:
                pair(p, False)
            pair(PAIRS - 1, True)
            sp.wait_ge(yg_added, 2 + CH * E)
            sp.dma_start(kst[1][3 * HD:3 * HD + 1, :, :].rearrange("p h t -> p (h t)").bitcast(fp32),
                         kst[0][3 * HD:3 * HD + 1, :, :].rearrange("p h t -> p (h t)").bitcast(fp32)
                         ).then_inc(ones_in, 16)

            def batch(b, first, last):
                def no(kind, j, k):
                    return find(first, last, kind, j, k)

                stack(b, no("k", 1, 0), 1)
                max_row(b, no("turn", 0, 0), 1)
                if not first:
                    store(b, no("out", 0, 0), 1)
                max_row(b, no("turn", 0, 1), 2)
                if not last:
                    stack(b, no("k", 1, 2), 0)
                max_row(b, no("turn", 0, 2), 3)
                if not last:
                    max_row(b, no("turn", 0, 3), 4)
                store(b, no("out", 0, 3), 0)

            sections(sp, batch)
            store(B - 1, LAST_OUT, 1)
            sp.wait_ge(out_done, 16 * CH)

        @block.gpsimd
        def _(pool):
            nc.gpsimd.memset(ident[:, :], 0.0).then_inc(zeroed, 1)
            nc.gpsimd.memset(ones[:, :], 1.0).then_inc(zeroed, 1)
            nc.gpsimd.iota(rank[:, :, :], pattern=[[0, TILES], [-1, E1]], base=2 * E1, channel_multiplier=0,
                           allow_small_or_imprecise_dtypes=True).then_inc(zeroed, 1)
            pool.wait_ge(zeroed, 3)
            nc.gpsimd.affine_select(out=ident[:, :], in_=ident[:, :], compare_op=ALU.not_equal, fill=1.0, base=0,
                                    pattern=[[-1, 128]], channel_multiplier=1).then_inc(ident_set, 1)
            pool.wait_ge(ident_set, 1)
            nc.gpsimd.memset(kst[0][3 * HD:3 * HD + 1, :, :].bitcast(fp32), 1.0).then_inc(stack_ones, 1)
            pool.sem_inc(yg_added, 2)
            pool.wait_ge(stack_ones, 1)
            pool.wait_ge(res_in, 16)

            def add_gated(m, k):
                pool.wait_ge(yg_done, 2 + m)
                pool.wait_ge(yg_added, 2 + m)
                cols = slice(W * (k % CH), W * (k % CH + 1))
                nc.gpsimd.tensor_tensor(acc[:, cols], acc[:, cols], yg[:, k % 2, :], ALU.add).then_inc(yg_added, 1)

            for k in range(ITEMS):
                add_gated(k, k)
                if k < CH:
                    cols = slice(W * k, W * (k + 1))
                    if k == 0:
                        pool.wait_ge(xlo_set, CH)
                        pool.wait_ge(gid_in, 16)
                    else:
                        pool.wait_ge(same_a, 3 * k)
                    nc.gpsimd.tensor_tensor(same[:, :], xhi[:, cols].bitcast(fp32), xlo[:, cols].bitcast(fp32),
                                            ALU.add).then_inc(same_a, 1)
                    pool.wait_ge(same_a, 3 * k + 1)
                    nc.gpsimd.tensor_tensor(same[:, :], same[:, :], gid[:, cols], ALU.mult).then_inc(same_a, 1)
                    pool.wait_ge(same_a, 3 * k + 2)
                    pool.wait_ge(yg_added, 3 + k)
                    nc.gpsimd.tensor_tensor(acc[:, cols], acc[:, cols], same[:, :], ALU.add).then_inc(same_a, 1)
                elif k == CH:
                    pool.wait_ge(same_a, 3 * CH)
            with pool.Fori(1, PAIRS) as p:
                for k in range(ITEMS):
                    add_gated(ITEMS * p + k, k)

            def pair_sum(i, k, j):
                J = 4 * i + j
                pool.wait_ge(exp_done, ST * i + 8 * j + 8)
                if not (k == "first" and j < 2):
                    pool.wait_ge(den_done, J - 1)
                a, c = P[(2 * j) % 4], P[(2 * j + 1) % 4]
                nc.gpsimd.tensor_tensor(Psum[j % 2][:, :, :], a[:, :, :], c[:, :, :], ALU.add).then_inc(psum_done, 1)

            def batch(b, first, last):
                for k in range(4):
                    for j in range(4):
                        pair_sum(4 * b + k, "first" if first and k == 0 else k, j)

            sections(pool, batch)

        @block.scalar
        def _(act):
            act.sem_inc(gelu_done, 4)
            def deviations(r):
                act.wait_ge(var_set, r + 1)
                tiles = slice(8 * r, 8 * r + 8)
                nc.scalar.activation(rstd[:, tiles], rstd[:, tiles], ACT.Sqrt).then_inc(std_set, 1)

            deviations(0)
            for c in range(CH):
                if c % 2 == 0 and c // 2 + 1 < 4:
                    deviations(c // 2 + 1)
                cols = slice(W * c, W * (c + 1))
                act.wait_ge(x_turned, c + 1)
                nc.scalar.copy(xhi[:, cols], aux[c % 2][:, :])
                if c >= 2:
                    act.wait_ge(logits_set, c - 1)
                nc.scalar.copy(xTf[:, c % 2, :], aux[c % 2][:, :]).then_inc(xT_copied, 1)
            act.wait_ge(shifted, 1)
            nc.scalar.activation(prob[:, :, :], prob[:, :, :], ACT.Exp).then_inc(exped, 1)

            def gelu(p, k, beside):
                m = ITEMS * p + k
                for c in range(FC):
                    u = FC * m + c
                    act.wait_ge(up_done, u + 1)
                    if c == 0:
                        act.wait_ge(down_done, m + 1)
                    act.wait_ge(hlo_done, u + 1)
                    src = up_ps[c][:, :]
                    nc.scalar.activation(h_hi[:, k % 2, c, :], src, ACT.Gelu)
                    nc.scalar.activation(hf[:, c % 2, :], src, ACT.Gelu).then_inc(gelu_done, 1)
                    for no, (kind, j) in beside[c]:
                        project(0, 0, kind, j, no)

            with act.Fori(0, PAIRS - 1) as p:
                for k in range(ITEMS):
                    gelu(p, k, [[]] * FC)

            def exps(b, first, last):
                for g, k, c, units in numbered(first, last):
                    i, start = 4 * b + k, first and k == 0
                    for h, us in enumerate(places(units)):
                        for kind, j, no in us:
                            project(b, g + 1, kind, j, no)
                        if h == G and c == 0 and not start:
                            copy_o(i - 1, first and k == 1)
                        if h == 1 and c == 3 and not start:
                            act.wait_ge(den_done, 4 * i)
                            nc.scalar.copy(rden[:, :], ps_d[:, :]).then_inc(den_copied, 1)
                        if h >= G:
                            continue
                        u = ST * k + G * c + h
                        act.wait_ge(st_ready, 4 * ST * b + u + 1)
                        if h == 0 and not (start and c < 4):
                            act.wait_ge(pv_done, 8 * i + c - 3)
                            act.wait_ge(psum_done, 4 * i + c // 2 - 1)
                        nc.scalar.activation(P[c % 4][:, h, :], st[u % 3][:, :], ACT.Exp,
                                             scale=SCALE).then_inc(exp_done, 1)

            def copy_o(i, start):
                act.wait_ge(pv_done, 8 * i + 8)
                if not start:
                    act.wait_ge(on_done, i)
                nc.scalar.copy(oT[:, :], ps_o[:, :]).then_inc(o_copied, 1)

            def project(b, g, kind, j, no):
                cols, par, bank = slice(W * j, W * (j + 1)), g % 2, no % AB
                if kind not in ("q", "k", "latent", "v"):
                    return
                act.wait_ge(aux_ready, AUX_BATCH * b + no + 1)
                if kind in ("q", "k"):
                    if j == 0 and g:
                        act.wait_ge(stacked[1 - par], STACK * (b + 1))
                    dst = q_hi if kind == "q" else k_hi
                    nc.scalar.copy(dst[:, cols], aux[bank][:, :]).then_inc(hi_done, 1)
                elif kind == "latent":
                    nc.scalar.copy(lat[:, cols], aux[bank][0:R, :]).then_inc(aux_free[bank], 1)
                else:
                    nc.scalar.copy(v[par][:, 4 * j:4 * j + 4, :],
                                   aux[bank][:, :].rearrange("p (t d) -> p t d", t=4)).then_inc(aux_free[bank], 1)

            for k in range(ITEMS):
                gelu(PAIRS - 1, k, places(BESIDE_EXPERTS[k], FC))
            act.wait_ge(yg_added, 2 + CH * E)
            sections(act, exps)
            act.wait_ge(pv_done, 8 * 4 * B)
            act.wait_ge(on_done, 4 * B - 1)
            nc.scalar.copy(oT[:, :], ps_o[:, :]).then_inc(o_copied, 1)
            act.wait_ge(den_done, 4 * 4 * B)
            nc.scalar.copy(rden[:, :], ps_d[:, :]).then_inc(den_copied, 1)

        @block.vector
        def _(dve):
            links = [0]

            def link(ins):
                links[0] += 1
                ins.then_inc(chain, 1)
                dve.wait_ge(chain, links[0])

            dve.sem_inc(hlo_done, 2)
            dve.sem_inc(yg_done, 1)

            def split_weights(e, par):
                dve.wait_ge(w_in, 32 * e + 32)
                nc.vector.tensor_copy(w1_hi[:, par, :], w1_f[:, :])
                nc.vector.tensor_copy(w2_hi[:, par, :, :], w2_f[:, :, :]).then_inc(w_hi_set, 1)
                dve.wait_ge(w_hi_set, e + 1)
                nc.vector.tensor_tensor(w1_lo[:, par, :], w1_f[:, :], w1_hi[:, par, :].bitcast(fp32), ALU.subtract)
                nc.vector.tensor_tensor(w2_lo[:, par, :, :], w2_f[:, :, :], w2_hi[:, par, :, :].bitcast(fp32),
                                        ALU.subtract).then_inc(w_split, 1)

            def moments(r):
                tiles = range(8 * r, 8 * r + 8)
                dve.wait_ge(x_in[r], 16)
                for t in tiles:
                    last = nc.vector.bn_stats(stats[:, t, :], x[:, t, :])
                link(last)
                for t in tiles:
                    last = nc.vector.bn_aggr(mv[:, t, :], stats[:, t, :])
                link(last)
                nc.vector.tensor_scalar(rstd[:, 8 * r:8 * r + 8], mv[:, 8 * r:8 * r + 8, 1], EPS, None,
                                        ALU.add).then_inc(var_set, 1)

            def invert_deviations(r):
                dve.wait_ge(std_set, r + 1)
                nc.vector.reciprocal(rstd[:, 8 * r:8 * r + 8], rstd[:, 8 * r:8 * r + 8]).then_inc(recip_set, 1)
                dve.wait_ge(recip_set, r + 1)

            def norm(c):
                for t in range(4 * c, 4 * c + 4):
                    last = nc.vector.tensor_scalar(x[:, t, :], x[:, t, :], mv[:, t, 0:1], rstd[:, t:t + 1],
                                                   ALU.subtract, ALU.mult)
                last.then_inc(xn_set, 1)

            def low_part(c):
                dve.wait_ge(xT_copied, c + 1)
                cols = slice(W * c, W * (c + 1))
                nc.vector.tensor_tensor(xlo[:, cols], aux[c % 2][:, :], xhi[:, cols].bitcast(fp32),
                                        ALU.subtract).then_inc(xlo_set, 1)

            def logits(c):
                dve.wait_ge(logits_set, c + 1)
                nc.vector.tensor_tensor(prob[:, 4 * c:4 * c + 4, :],
                                        (ps_o, ps_d)[c % 2][:, 0:4 * E1].rearrange("p (t e) -> p t e", t=4),
                                        rb[:, :, :], ALU.add).then_inc(logits_read, 1)

            moments(0)
            for r in range(4):
                if r + 1 < 4:
                    moments(r + 1)
                if r == 0:
                    dve.wait_ge(const_in, CONSTS)
                invert_deviations(r)
                for c in (2 * r, 2 * r + 1):
                    norm(c)
                    if c >= 1:
                        low_part(c - 1)
                    if c >= 2:
                        logits(c - 2)
            low_part(CH - 1)
            split_weights(0, 0)
            logits(CH - 2)
            logits(CH - 1)
            dve.wait_ge(logits_read, CH)

            wide = [128, TILES, E1]
            bc = top[:, :].unsqueeze(2).to_broadcast(wide)
            link(nc.vector.reduce_max(top[:, :], prob[:, :, :], AX.X))
            nc.vector.tensor_tensor(prob[:, :, :], prob[:, :, :], bc, ALU.subtract).then_inc(shifted, 1)
            dve.wait_ge(exped, 1)
            link(nc.vector.reduce_sum(top[:, :], prob[:, :, :], AX.X))
            link(nc.vector.reciprocal(top[:, :], top[:, :]))
            link(nc.vector.tensor_tensor(prob[:, :, :], prob[:, :, :], bc, ALU.mult))
            dve.wait_ge(ident_set, 1)

            def choose(src, onehot):
                link(nc.vector.reduce_max(top[:, :], src, AX.X))
                link(nc.vector.tensor_tensor(key[:, :, :], src, bc, ALU.is_equal))
                link(nc.vector.tensor_tensor(key[:, :, :], key[:, :, :], rank[:, :, :], ALU.mult))
                link(nc.vector.reduce_max(top[:, :], key[:, :, :], AX.X))
                link(nc.vector.tensor_tensor(onehot, key[:, :, :], bc, ALU.is_equal))

            choose(prob[:, :, :], pick[:, :, :])
            link(nc.vector.scalar_tensor_tensor(out=left[:, :, :], in0=pick[:, :, :], scalar=-2.0,
                                                in1=prob[:, :, :], op0=ALU.mult, op1=ALU.add))
            choose(left[:, :, :], key[:, :, :])
            link(nc.vector.tensor_tensor(key[:, :, :], key[:, :, :], pick[:, :, :], ALU.add))
            nc.vector.tensor_tensor(gates[:, :, :].rearrange("p e t -> p t e"), prob[:, :, :], key[:, :, :],
                                    ALU.mult).then_inc(gates_set, 1)
            dve.wait_ge(gates_set, 1)
            nc.vector.transpose(gatesT[:, :, :].rearrange("p e t -> p (e t)"),
                                gates[:, :, :].rearrange("p e t -> p (e t)")).then_inc(gatesT_set, 1)
            link(nc.vector.tensor_copy(wq_hi[:, :], wq_f[:, :]))
            link(nc.vector.tensor_copy(wd_hi[:, :], wd_f[:, :]))
            link(nc.vector.tensor_tensor(wq_lo[:, :], wq_f[:, :], wq_hi[:, :].bitcast(fp32), ALU.subtract))
            link(nc.vector.tensor_tensor(wd_lo[:, :], wd_f[:, :], wd_hi[:, :].bitcast(fp32), ALU.subtract))

            def gate(p, k):
                m, par, i = ITEMS * p + k, k // CH, k % CH
                dve.wait_ge(down_done, 3 + m)
                dve.wait_ge(yg_added, 1 + m)
                half, at = i // (CH // 2), W * (i % (CH // 2))
                if at == 0:
                    dve.wait_ge(gbc_in[half], 16 * (2 * p + par) + 16)
                nc.vector.tensor_tensor(yg[:, k % 2, :], ps_o[:, :], gbc[:, half, at:at + W],
                                        ALU.mult).then_inc(yg_done, 1)

            def pair(p, last):
                for k in range(ITEMS):
                    m = ITEMS * p + k
                    beside = places(BESIDE_EXPERTS[k] if last else [], FC)
                    for c in range(FC):
                        dve.wait_ge(gelu_done, 4 + FC * m + c + 1)
                        nc.vector.tensor_tensor(h_lo[:, k % 2, c, :], hf[:, c % 2, :],
                                                h_hi[:, k % 2, c, :].bitcast(fp32), ALU.subtract).then_inc(hlo_done, 1)
                        if c == 1 and k:
                            gate(p, k - 1)
                        for no, (kind, j) in beside[c]:
                            unit(0, 0, 0, kind, j, no)
                    if k % CH == 2 and not (last and k > CH):
                        split_weights(2 * p + k // CH + 1, (k // CH + 1) % 2)
                gate(p, ITEMS - 1)

            def unit(b, g, k, kind, j, no):
                bank = no % AB
                if kind in ("max", "turn", "out"):
                    dve.wait_ge(aux_ready, AUX_BATCH * b + no + 1)
                if kind == "max":
                    nc.vector.reduce_max(halfmax[:, k % 2, j // 2, j % 2:j % 2 + 1], aux[bank][:, :],
                                         AX.X).then_inc(aux_free[bank], 1)
                    if j == 2 * 4 * G - 1:
                        wait_unit_read(dve, b, no - 1)
                        wait_unit_read(dve, b, no)
                        nc.vector.tensor_tensor(qmax[:, k % 2, :], halfmax[:, k % 2, :, 0], halfmax[:, k % 2, :, 1],
                                                ALU.max).then_inc(qmax_done, 1)
                elif kind == "turn":
                    if not (isinstance(b, int) and b == 0 and k < 2):
                        dve.wait_ge(max_in[k % 2], 16 * (2 * b + k // 2))
                    nc.vector.tensor_scalar(maxT[:, k % 2, :], aux[bank][0:G * 4, 0:128], -1.0, None,
                                            ALU.mult).then_inc(aux_free[bank], 1)
                elif kind in ("q", "k"):
                    hi, lo = (q_hi, q_lo) if kind == "q" else (k_hi, k_lo)
                    dve.wait_ge(hi_done, 4 * (2 * b + g) + 2 * j + (1 if kind == "q" else 2))
                    cols = slice(W * j, W * (j + 1))
                    nc.vector.tensor_tensor(lo[:, cols], aux[bank][:, :], hi[:, cols].bitcast(fp32),
                                            ALU.subtract).then_inc(aux_free[bank], 1)
                elif kind == "out":
                    add(b, k - 2, bank)

            def invert(i, q):
                if q == 0:
                    dve.wait_ge(den_copied, i + 1)
                cols = slice(128 * q, 128 * q + 128)
                ins = nc.vector.reciprocal(rden[:, cols], rden[:, cols])
                if q == 3:
                    ins.then_inc(rec_done, 1)

            def normalise(i):
                dve.wait_ge(rec_done, i + 1)
                dve.wait_ge(o_copied, i + 1)
                nc.vector.tensor_tensor(on[:, :], oT[:, :], rden[:, :], ALU.mult).then_inc(on_done, 1)

            def add(b, k, bank):
                cols = bass.ds(T * b + W * (k % 2), W) if k >= 0 else bass.ds(T * b - W, W)
                nc.vector.tensor_tensor(acc[:, cols], acc[:, cols], aux[bank][:, :],
                                        ALU.add).then_inc(aux_free[bank], 1)

            def batch(b, first, last):
                for g, k, c, units in numbered(first, last):
                    i, start = 4 * b + k, first and k == 0
                    for q, us in enumerate(places(units)):
                        for kind, j, no in us:
                            unit(b, g + 1, k + 1, kind, j, no)
                        if q == 3 and 3 <= c < 7 and not start:
                            invert(i - 1, c - 3)
                    if c == 6 and not start:
                        normalise(i - 1)

            with dve.Fori(0, PAIRS - 1) as p:
                pair(p, False)
            pair(PAIRS - 1, True)
            sections(dve, batch)
            i = 4 * B - 1
            for q in range(4):
                invert(i, q)
            normalise(i)
            unit(B - 1, 2, 5, "out", 0, LAST_OUT)

        @block.tensor
        def _(pe):
            pe.sem_inc(down_done, 2)
            pe.wait_ge(ident_set, 1)
            pe.wait_ge(const_in, CONSTS)
            def router(c):
                pe.wait_ge(xT_copied, c + 1)
                for q in range(4):
                    last = nc.tensor.matmul((ps_o, ps_d)[c % 2][:, E1 * q:E1 * (q + 1)],
                                            xTf[:, c % 2, 128 * q:128 * q + 128], rw[:, :], start=True, stop=True)
                last.then_inc(logits_set, 1)

            for c in range(CH):
                pe.wait_ge(xn_set, c + 1)
                if c >= 2:
                    pe.wait_ge(xlo_set, c - 1)
                for q in range(4):
                    last = nc.tensor.transpose(aux[c % 2][:, 128 * q:128 * q + 128], x[:, 4 * c + q, :], ident[:, :])
                last.then_inc(x_turned, 1)
                if c >= 1:
                    if c >= 3:
                        pe.wait_ge(logits_read, c - 2)
                    router(c - 1)
            pe.wait_ge(logits_read, CH - 2)
            router(CH - 1)
            pe.wait_ge(xlo_set, CH)

            def up(p, k, beside):
                m, i, par = ITEMS * p + k, k % CH, k // CH
                if i == 0:
                    pe.wait_ge(w_split, 2 * p + par + 1)
                cols = slice(W * i, W * (i + 1))
                for c in range(FC):
                    if c == FC - 1 and k == 0:
                        pe.wait_ge(logits_read, CH)
                    pe.wait_ge(gelu_done, FC * m + c + 1)
                    w = slice(128 * c, 128 * c + 128)
                    split3(up_ps[c][:, :], w1_hi[:, par, w], w1_lo[:, par, w], xhi[:, cols], xlo[:, cols],
                           True, True).then_inc(up_done, 1)
                    for no, (kind, j) in beside[c]:
                        unit(0, 0, 0, kind, j, no)

            def down(p, k):
                m, par = ITEMS * p + k, k // CH
                pe.wait_ge(yg_done, m + 1)
                for c in range(FC):
                    pe.wait_ge(hlo_done, 2 + FC * m + c + 1)
                    last = split3(ps_o[:, :], w2_hi[:, par, c, :], w2_lo[:, par, c, :], h_hi[:, k % 2, c, :],
                                  h_lo[:, k % 2, c, :], c == 0, c == FC - 1)
                last.then_inc(down_done, 1)

            def unit(b, g, k, kind, j, no):
                out, par, b_of = aux[no % AB], g % 2, b + g // 2
                if not (g == 0 and no < AB):
                    wait_unit_read(pe, b, no - AB)
                cols = slice(W * j, W * (j + 1))
                if kind == "max":
                    hh, qt, kh = j // 8, (j // 2) % 4, j % 2
                    gp, half = (k // 2) % 2, k % 2
                    if j == 0:
                        pe.wait_ge(stacked[gp], STACK * (b + k // 4 + 1))
                        if k == 0:
                            pe.wait_ge(stack_ones, 1)
                        elif k == 2 and isinstance(b, int) and b == 0:
                            pe.wait_ge(ones_in, 16)
                    q0 = 128 * qt
                    nc.tensor.matmul(out[:, :], qst[gp][0:3 * HD, half, hh, q0:q0 + 128],
                                     kst[gp][0:3 * HD, hh, W * kh:W * kh + W], start=True,
                                     stop=True).then_inc(aux_ready, 1)
                elif kind == "turn":
                    pe.wait_ge(qmax_done, 4 * b + k + 1)
                    nc.tensor.transpose(out[0:G * 4, 0:128], qmax[:, k % 2, :], ident[:, :]).then_inc(aux_ready, 1)
                elif kind == "out":
                    pe.wait_ge(on_done, 4 * b + k - 1)
                    nc.tensor.matmul(out[:, :], wo[:, ((k - 2) % 4) // 2, :], on[:, :], start=True,
                                     stop=True).then_inc(aux_ready, 1)
                elif kind == "latent":
                    toks = bass.ds(T * b_of + W * j, W)
                    split3(out[0:R, :], wd_hi[:, :], wd_lo[:, :], xhi[:, toks], xlo[:, toks], True,
                           True).then_inc(aux_ready, 1)
                elif kind == "q":
                    toks = bass.ds(T * b_of + W * j, W)
                    w = slice(128 * par, 128 * par + 128)
                    split3(out[:, :], wq_hi[:, w], wq_lo[:, w], xhi[:, toks], xlo[:, toks], True,
                           True).then_inc(aux_ready, 1)
                elif kind == "k":
                    nc.tensor.matmul(out[:, :], wk[:, 128 * par:128 * par + 128], lat[:, cols], start=True,
                                     stop=True).then_inc(aux_ready, 1)
                else:
                    for q in range(4):
                        t = 4 * j + q
                        last = nc.tensor.matmul(out[:, 128 * q:128 * q + 128], lat[:, 128 * t:128 * t + 128],
                                                wv[:, 128 * par:128 * par + 128], start=True, stop=True)
                    last.then_inc(aux_ready, 1)

            def scores(b, k, c, h, first):
                gp, half, u = k // 2, k % 2, ST * k + G * c + h
                if not (first and u < 3):
                    pe.wait_ge(exp_done, 4 * ST * b + {0: -2, 1: -1, 2: -3}.get(u, u - 3) + 1)
                if c == 0 and h == 0:
                    pe.wait_ge(max_in[k % 2], 16 * (2 * b + k // 2 + 1))
                nc.tensor.matmul(st[u % 3][:, :], kst[gp][:, h, 128 * c:128 * c + 128], qst[gp][:, half, h, :],
                                 start=True, stop=True).then_inc(st_ready, 1)

            def values(i, k, c, start):
                pe.wait_ge(exp_done, ST * i + G * c + G)
                gp = k // 2
                if c == 0:
                    if not start:
                        pe.wait_ge(o_copied, i)
                for h in range(G):
                    rows = slice(HD * h, HD * (h + 1))
                    last = nc.tensor.matmul(ps_o[rows, :], v[gp][:, c, rows], P[c % 4][:, h, :], start=(c == 0),
                                            stop=(c == KC - 1), skip_group_check=True)
                last.then_inc(pv_done, 1)

            def denominators(i, j, start):
                pe.wait_ge(psum_done, 4 * i + j + 1)
                if j == 0 and not start:
                    pe.wait_ge(den_copied, i)
                for h in range(G):
                    rows = slice(HD * h, HD * (h + 1))
                    last = nc.tensor.matmul(ps_d[rows, :], ones[:, :], Psum[j % 2][:, h, :], start=(j == 0), stop=(j == 3),
                                            skip_group_check=True)
                last.then_inc(den_done, 1)

            def lagging(i, k, c, first):
                k1 = (k - 1) % 4
                if c == 0:
                    if not first:
                        values(i - 1, k1, KC - 1, False)
                else:
                    values(i, k, c - 1, first)

            def sums(i, k, c, first):
                if c in (4, 6):
                    denominators(i, c // 2 - 2, first)
                if c in (0, 2) and not first:
                    denominators(i - 1, c // 2 + 2, False)

            def batch(b, first, last):
                for g, k, c, units in numbered(first, last):
                    i, start = 4 * b + k, first and k == 0
                    for place, us in enumerate(places(units)):
                        for kind, j, no in us:
                            unit(b, g + 1, k + 1, kind, j, no)
                        if place < G:
                            scores(b, k, c, place, first)
                        elif place == G:
                            lagging(i, k, c, start)
                        else:
                            sums(i, k, c, start)

            def pair(p, last):
                for k in range(ITEMS):
                    up(p, k, places(BESIDE_EXPERTS[k] if last else [], FC))
                    if k:
                        down(p, k - 1)
                down(p, ITEMS - 1)

            with pe.Fori(0, PAIRS - 1) as p:
                pair(p, False)
            pair(PAIRS - 1, True)
            pe.wait_ge(yg_done, 1 + E * CH)
            sections(pe, batch)
            i = 4 * B - 1
            values(i, 3, KC - 1, False)
            denominators(i, 2, False)
            denominators(i, 3, False)
            unit(B - 1, 2, 5, "out", 0, LAST_OUT)


def kernel(L0_attn_x, L0_attn_Wq, L0_attn_Wkv_down, L0_attn_Wk_up, L0_attn_Wv_up, L0_attn_Wo, L0_ffn_router_w,
           L0_ffn_router_b, L0_ffn_w1, L0_ffn_w2):
    import numpy as np
    import concourse.bacc as bacc
    from concourse.bass_utils import run_bass_kernel_spmd

    x = np.ascontiguousarray(L0_attn_x).reshape(N, D)
    arrays = {
        "x_dram": x,
        "xT_dram": np.ascontiguousarray(x.T),
        "wqT_dram": np.ascontiguousarray(np.asarray(L0_attn_Wq).T),
        "wdT_dram": np.ascontiguousarray(np.asarray(L0_attn_Wkv_down).T),
        "wkT_dram": np.ascontiguousarray(np.asarray(L0_attn_Wk_up).T),
        "wvT_dram": np.ascontiguousarray(np.asarray(L0_attn_Wv_up).T),
        "woT_dram": np.ascontiguousarray(np.asarray(L0_attn_Wo).T),
        "rw_dram": np.ascontiguousarray(L0_ffn_router_w),
        "rb_dram": np.ascontiguousarray(L0_ffn_router_b),
        "w1_dram": np.ascontiguousarray(L0_ffn_w1),
        "w2_dram": np.ascontiguousarray(L0_ffn_w2),
    }
    nc = bacc.Bacc("TRN2", target_bir_lowering=False, num_devices=1)
    ins = [nc.dram_tensor(k, a.shape, mybir.dt.from_np(a.dtype), kind="ExternalInput").ap()
           for k, a in arrays.items()]
    out = nc.dram_tensor("outT", (D, N), fp32, kind="ExternalOutput").ap()
    build(nc, *ins, out)
    r = run_bass_kernel_spmd(nc, [arrays], core_ids=[0])
    return np.ascontiguousarray(np.asarray(r.results[0]["outT"]).T).reshape(B, T, D)
```

```python
import concourse.bass as bass
from concourse import mybir
from contextlib import ExitStack

B, T, D = 4, 1024, 128
H, HD, R = 8, 32, 64
E, F = 8, 512
N = B * T
W = 512
CH = N // W
TILES = N // 128
G = 4
KC = T // 128
FC = F // 128
E1 = E + 1
EPS = 1e-5
SCALE = HD ** -0.5

fp32 = mybir.dt.float32
f32r = mybir.dt.float32r
ALU = mybir.AluOpType
ACT = mybir.ActivationFunctionType
AX = mybir.AxisListType

AB = 3
EARLY = 4
AHEAD = [("early", u) for u in range(EARLY)]
MAXES = [("max", u) for u in range(EARLY, G * 4 * 2)]


def projections(latent):
    lat = [("latent", j) for j in range(2)] if latent else []
    return lat + [(k, j) for k in ("q", "k") for j in range(2)]


VALUES = [("v", j) for j in range(2)]


def cut(units, sizes):
    out, at = [], 0
    for s in sizes:
        out.append(units[at:at + s])
        at += s
    assert at == len(units)
    return out


def group_steps(g, last):
    nxt = not (last and g == 1)
    qk = projections(latent=(g == 1)) if nxt else []
    vs = VALUES if nxt else []
    n = len(qk)
    one = cut(qk + MAXES, [n, 4, 5, 4, 4, 5, 6, 0])
    one[6] += vs[:1]
    one[7] = [("turn", 0)] + (AHEAD[:2] if nxt else []) + [("out", 0)] + vs[1:] + (AHEAD[2:] if nxt else [])
    if nxt:
        two = cut(MAXES, [3, 4, 5, 4, 4, 4, 4, 0])
        two[6] += AHEAD[:1]
        two[7] = [("turn", 0)] + AHEAD[1:3] + [("out", 0)] + AHEAD[3:]
    else:
        two = [[] for _ in range(7)] + [[("out", 0)]]
    return one + two


PROLOGUE = (projections(latent=True) + VALUES + [("max", u) for u in range(G * 4 * 2)]
            + AHEAD[:2] + [("turn", 0)] + AHEAD[2:])
BESIDE_EXPERTS = cut(list(enumerate(PROLOGUE)), [0, 4, 2, 2, 0, 0, 1] + [4] * 9)
AUX_BATCH = sum(len(s) for g in range(2) for s in group_steps(g, False))
assert AUX_BATCH % AB == 0


def numbered(first, last):
    at = len(PROLOGUE) - (not first)
    for g in range(2):
        for s, units in enumerate(group_steps(g, last)):
            k, out = 2 * g + s // 8, []
            for kind, j in units:
                if not (first and k == 0 and kind == "out"):
                    out.append((kind, j, at))
                    at += 1
            yield g, k, s % 8, out


LAST_OUT = max(no for _, _, _, us in numbered(False, True) for _, _, no in us) + 1


def places(units, n=6):
    return [units[len(units) * j // n:len(units) * (j + 1) // n] for j in range(n)]


def beside_item(k, last):
    units = BESIDE_EXPERTS[k] if last else []
    return places(units, FC) + [[]] * FC if k == 2 * CH - 1 else places(units, 2 * FC)


def find(first, last, kind, j, k):
    return next(no for _, kk, _, us in numbered(first, last) for t, jj, no in us if (t, jj, kk) == (kind, j, k))


def build(nc, xn_d, xT_d, wqT_d, wdT_d, wkT_d, wvT_d, woT_d, rw_d, rb_d, w1_d, w2_d, out_d):
    gates_d = nc.dram_tensor("gates_d", (E1, 128, N // 128), fp32, kind="Internal").ap()
    ctx = ExitStack()
    with ctx:
        def sb(name, shape, dt=fp32, at=ctx):
            return at.enter_context(nc.sbuf_tensor(name, shape, dt))

        def sem(name):
            return ctx.enter_context(nc.semaphore(name))

        ident = sb("ident", [128, 128])
        ones = sb("ones", [128, HD])
        xhi = sb("xhi", [D, N], f32r)
        xlo = sb("xlo", [D, N], f32r)
        acc = sb("acc", [D, N])
        wq_f = sb("wq_f", [D, H * HD])
        wq_hi = sb("wq_hi", [D, H * HD], f32r)
        wq_lo = sb("wq_lo", [D, H * HD], f32r)
        wd_f = sb("wd_f", [D, R])
        wd_hi = sb("wd_hi", [D, R], f32r)
        wd_lo = sb("wd_lo", [D, R], f32r)
        wk = sb("wk", [R, H * HD])
        wv = sb("wv", [R, H * HD])
        wo = sb("wo", [128, 2, D])

        def stacks(i):
            return (sb(f"qst{i}", [3 * HD + 1, 2, G, W], f32r), sb(f"kst{i}", [3 * HD + 1, G, T], f32r))

        warm = sb("warm", [128, 1])
        early = stacks(0)
        lat = sb("lat", [R, T])
        v = [sb(f"v{i}", [128, KC, 128]) for i in range(2)]
        halfmax = sb("halfmax", [128, 2, G * 4, 2])
        qmax = sb("qmax", [128, 2, G * 4])
        maxT = sb("maxT", [G * 4, 2, 128], f32r)

        with ExitStack() as part:
            gid = sb("gid", [128, N], at=part)
        q_hi = sb("q_hi", [128, T], f32r)
        q_lo = sb("q_lo", [128, T], f32r)
        k_hi = sb("k_hi", [128, T], f32r)
        k_lo = sb("k_lo", [128, T], f32r)

        with ExitStack() as part:
            mv = sb("mv", [128, TILES, 2], at=part)
            rstd = sb("rstd", [128, TILES], at=part)
            shift = sb("shift", [128, TILES], at=part)
            rw = sb("rw", [D, 32], at=part)
            rb = sb("rb", [128, E1], at=part)
            prob = sb("prob", [128, TILES, E1], at=part)
            key = sb("key", [128, TILES, E1], at=part)
            pick = sb("pick", [128, TILES, E1], at=part)
            left = sb("left", [128, TILES, E1], at=part)
            rank = sb("rank", [128, TILES, E1], at=part)
            top = sb("top", [128, TILES], at=part)
            gates = sb("gates", [128, E1, TILES], at=part)
            gatesT = sb("gatesT", [128, E1, 32], at=part)
            gbc = sb("gbc", [128, 2, N // 2], at=part)
            w1_f = sb("w1_f", [D, F], at=part)
            w2_f = sb("w2_f", [128, FC, D], at=part)
            w1_hi = sb("w1_hi", [D, 2, F], f32r, at=part)
            w1_lo = sb("w1_lo", [D, 2, F], f32r, at=part)
            w2_hi = sb("w2_hi", [128, 2, FC, D], f32r, at=part)
            w2_lo = sb("w2_lo", [128, 2, FC, D], f32r, at=part)
            hf = sb("hf", [128, 2, W], at=part)
            yg = sb("yg", [D, 2, W], at=part)
            same = sb("same", [D, W], at=part)
            with ExitStack() as norm_part:
                x = sb("x", [128, TILES, D], at=norm_part)
                stats = sb("stats", [128, TILES, 6], at=norm_part)
                xTf = sb("xTf", [D, 2, W], at=norm_part)
                logitsT = sb("logitsT", [128, 2, W // 32, 32], at=norm_part)
            h_hi = sb("h_hi", [128, 2, FC, W], f32r, at=part)
            h_lo = sb("h_lo", [128, 2, FC, W], f32r, at=part)

        late = stacks(1)
        qst, kst = (early[0], late[0]), (early[1], late[1])
        P = [sb(f"P{i}", [128, G, W]) for i in range(4)]
        Psum = [sb(f"Psum{i}", [128, G, W]) for i in range(2)]
        oT = sb("oT", [128, W])
        denT = sb("denT", [128, W])
        rsmall = sb("rsmall", [128, W // 32])
        rden = sb("rden", [128, W])
        on = sb("on", [128, W])

        st = [ctx.enter_context(nc.psum_tensor(f"st{i}", [128, W], fp32)) for i in range(3)]
        aux = [ctx.enter_context(nc.psum_tensor(f"aux{i}", [128, W], fp32)) for i in range(AB)]
        ps_o = ctx.enter_context(nc.psum_tensor("ps_o", [128, W], fp32))
        ps_d = ctx.enter_context(nc.psum_tensor("ps_d", [128, W], fp32))
        up_ps = st + [ps_d]

        x_in = [sem(f"x_in{i}") for i in range(4)]
        res_in = sem("res_in")
        const_in = sem("const_in")
        zeroed = sem("zeroed")
        ident_set = sem("ident_set")
        chain = sem("chain")
        var_set = sem("var_set")
        std_set = sem("std_set")
        xn_act = sem("xn_act")
        xn_dve = sem("xn_dve")
        recip_set = sem("recip_set")
        x_turned = sem("x_turned")
        xT_copied = sem("xT_copied")
        xlo_set = sem("xlo_set")
        logits_set = sem("logits_set")
        logits_read = sem("logits_read")
        w_hi_set = sem("w_hi_set")
        proj_hi_set = sem("proj_hi_set")
        proj_split = sem("proj_split")
        shifted = sem("shifted")
        exped = sem("exped")
        gates_set = sem("gates_set")
        gatesT_set = sem("gatesT_set")
        gates_out = sem("gates_out")
        gid_in = sem("gid_in")
        w_in = sem("w_in")
        gbc_in = [sem(f"gbc_in{i}") for i in range(2)]
        w_split = sem("w_split")
        up_done = sem("up_done")
        gelu_done = sem("gelu_done")
        hlo_done = sem("hlo_done")
        down_done = sem("down_done")
        yg_done = sem("yg_done")
        yg_added = sem("yg_added")
        same_a = sem("same_a")
        stack_ones = sem("stack_ones")
        ones_in = sem("ones_in")
        aux_ready = sem("aux_ready")
        aux_free = [sem(f"aux_free{i}") for i in range(AB)]
        hi_done = sem("hi_done")
        qmax_done = sem("qmax_done")
        stacked = [sem(f"stacked{i}") for i in range(2)]
        max_in = [sem(f"max_in{i}") for i in range(2)]
        st_ready = sem("st_ready")
        exp_done = sem("exp_done")
        pv_done = sem("pv_done")
        psum_done = sem("psum_done")
        last_psum = sem("last_psum")
        den_done = sem("den_done")
        den_read = sem("den_read")
        rec_done = sem("rec_done")
        rden_set = sem("rden_set")
        o_copied = sem("o_copied")
        on_done = sem("on_done")
        out_done = sem("out_done")

        PAIRS = E // 2
        ITEMS = 2 * CH
        STACK = 16 * 6 * G
        CONSTS = 16 * 7

        def split3(out, w_hi, w_lo, m_hi, m_lo, start, stop):
            nc.tensor.matmul(out, w_hi, m_lo, start=start, stop=False)
            nc.tensor.matmul(out, w_lo, m_hi, start=False, stop=False)
            return nc.tensor.matmul(out, w_hi, m_hi, start=False, stop=stop)

        def sections(eng, batch):
            batch(0, True, False)
            with eng.Fori(1, B - 1) as b:
                batch(b, False, False)
            batch(B - 1, False, True)

        SUMS = KC - 2

        def absorbed(c):
            return (1, 1, 2, 3, 4, 4, 5, 6)[c]

        ST = G * KC

        def units_read(b, no):
            return AUX_BATCH // AB * b + no // AB + 1

        def wait_unit_read(eng, b, no):
            eng.wait_ge(aux_free[no % AB], units_read(b, no))

        block = ctx.enter_context(nc.Block())

        @block.sync
        def _(sp):
            xv = xn_d.rearrange("(t p) d -> p t d", p=128)
            for i in range(4):
                sp.dma_start(x[:, 8 * i:8 * i + 8, :], xv[:, 8 * i:8 * i + 8, :]).then_inc(x_in[i], 16)
            sp.wait_ge(zeroed, 4)
            sp.dma_start(rw[:, 0:E1], rw_d).then_inc(const_in, 16)
            sp.dma_start(rb[:, :], rb_d.partition_broadcast(128)).then_inc(const_in, 16)
            sp.dma_start(wq_f[:, :], wqT_d).then_inc(const_in, 16)
            sp.dma_start(wd_f[:, :], wdT_d).then_inc(const_in, 16)
            sp.dma_start(wk[:, :], wkT_d).then_inc(const_in, 16)
            sp.dma_start(wv[:, :], wvT_d).then_inc(const_in, 16)
            sp.dma_start(wo[:, :, :], woT_d.rearrange("(g p) d -> p g d", p=128)).then_inc(const_in, 16)
            sp.dma_start(w1_f[:, :], w1_d[0]).then_inc(w_in, 16)
            sp.dma_start(w2_f[:, :, :], w2_d[0].rearrange("(c p) d -> p c d", p=128)).then_inc(w_in, 16)
            sp.dma_start(acc[:, :], xT_d).then_inc(res_in, 16)
            def load_weights(e):
                sp.wait_ge(w_split, e)
                sp.dma_start(w1_f[:, :], w1_d[bass.ds(e, 1)].rearrange("e d f -> d (e f)")).then_inc(w_in, 16)
                sp.dma_start(w2_f[:, :, :],
                             w2_d[bass.ds(e, 1)].rearrange("e (c p) d -> p (e c) d", p=128)).then_inc(w_in, 16)

            load_weights(1)
            sp.wait_ge(gatesT_set, 1)
            sp.dma_start(gates_d.rearrange("e p t -> p e t"), gatesT[:, :, :]).then_inc(gates_out, 16)
            sp.wait_ge(gates_out, 16)
            rows = gates_d.rearrange("e p t -> e (p t)")

            def load_gates(e, half):
                src = rows[bass.ds(e, 1), N // 2 * half:N // 2 * (half + 1)].rearrange("e n -> (e n)")
                sp.dma_start(gbc[:, half, :], src.partition_broadcast(128)).then_inc(gbc_in[half], 16)

            load_gates(0, 0)
            sp.dma_start(gid[:, :], rows[E].partition_broadcast(128)).then_inc(gid_in, 16)
            load_gates(0, 1)

            def pair(p, last):
                for j in range(2):
                    e = 2 * p + j
                    if last and j == 1:
                        max_row(0, PROLOGUE.index(("turn", 0)), 0)
                        break
                    if not last:
                        load_weights(e + 2)
                    else:
                        stack(0, PROLOGUE.index(("k", 1)), 0)
                    for half in range(2):
                        sp.wait_ge(yg_done, 1 + CH * e + CH // 2 * (half + 1))
                        load_gates(e + 1, half)

            def held(value):
                return value if isinstance(value, int) else sp.snap(value)

            def stack(b, no, par):
                wait_unit_read(sp, b, no)
                for h in range(G):
                    rows = slice(HD * h, HD * (h + 1))
                    for r, src in enumerate((k_hi, k_lo, k_hi)):
                        sp.dma_start(kst[par][HD * r:HD * (r + 1), h, :].bitcast(fp32),
                                     src[rows, :].bitcast(fp32)).then_inc(stacked[par], 16)
                    for r, src in enumerate((q_hi, q_hi, q_lo)):
                        sp.dma_start(qst[par][HD * r:HD * (r + 1), :, h, :].bitcast(fp32),
                                     src[rows, :].rearrange("p (a w) -> p a w", a=2)
                                     .bitcast(fp32)).then_inc(stacked[par], 16)

            def max_row(b, no, k):
                wait_unit_read(sp, b, no)
                par, half = (k % 4) // 2, k % 2
                sp.dma_start(qst[par][3 * HD:3 * HD + 1, half, :, :].rearrange("p h w -> p (h w)").bitcast(fp32),
                             maxT[:, k % 2, :].bitcast(fp32)).then_inc(max_in[k % 2], 16)

            def store(b, no, half):
                at = T * b + W * half if half == 0 or no == LAST_OUT else T * b - W
                at, count = held(at), held(units_read(b, no))
                sp.wait_ge(aux_free[no % AB], count)
                sp.dma_start(out_d[:, bass.ds(at, W)], acc[:, bass.ds(at, W)]).then_inc(out_done, 16)

            with sp.Fori(0, PAIRS - 1) as p:
                pair(p, False)
            pair(PAIRS - 1, True)
            sp.wait_ge(yg_added, 2 + CH * E)
            sp.dma_start(kst[1][3 * HD:3 * HD + 1, :, :].rearrange("p h t -> p (h t)").bitcast(fp32),
                         kst[0][3 * HD:3 * HD + 1, :, :].rearrange("p h t -> p (h t)").bitcast(fp32)
                         ).then_inc(ones_in, 16)

            def batch(b, first, last):
                def no(kind, j, k):
                    return find(first, last, kind, j, k)

                stack(b, no("k", 1, 0), 1)
                max_row(b, no("turn", 0, 0), 1)
                if not first:
                    store(b, no("out", 0, 0), 1)
                max_row(b, no("turn", 0, 1), 2)
                if not last:
                    stack(b, no("k", 1, 2), 0)
                max_row(b, no("turn", 0, 2), 3)
                if not last:
                    max_row(b, no("turn", 0, 3), 4)
                store(b, no("out", 0, 3), 0)

            sections(sp, batch)
            store(B - 1, LAST_OUT, 1)
            sp.wait_ge(out_done, 16 * CH)

        @block.gpsimd
        def _(pool):
            nc.gpsimd.memset(ident[:, :], 0.0).then_inc(zeroed, 1)
            nc.gpsimd.memset(rw[:, :], 0.0).then_inc(zeroed, 1)
            nc.gpsimd.memset(ones[:, :], 1.0).then_inc(zeroed, 1)
            nc.gpsimd.iota(rank[:, :, :], pattern=[[0, TILES], [-1, E1]], base=2 * E1, channel_multiplier=0,
                           allow_small_or_imprecise_dtypes=True).then_inc(zeroed, 1)
            pool.wait_ge(zeroed, 4)
            nc.gpsimd.affine_select(out=ident[:, :], in_=ident[:, :], compare_op=ALU.not_equal, fill=1.0, base=0,
                                    pattern=[[-1, 128]], channel_multiplier=1).then_inc(ident_set, 1)
            pool.wait_ge(w_in, 32)
            nc.gpsimd.tensor_copy(w1_hi[:, 0, :], w1_f[:, :])
            nc.gpsimd.tensor_copy(w2_hi[:, 0, :, :], w2_f[:, :, :]).then_inc(w_hi_set, 1)
            pool.wait_ge(w_hi_set, 1)
            nc.gpsimd.tensor_tensor(w1_lo[:, 0, :], w1_f[:, :], w1_hi[:, 0, :].bitcast(fp32), ALU.subtract)
            nc.gpsimd.tensor_tensor(w2_lo[:, 0, :, :], w2_f[:, :, :], w2_hi[:, 0, :, :].bitcast(fp32),
                                    ALU.subtract).then_inc(w_split, 1)
            pool.wait_ge(const_in, CONSTS)
            nc.gpsimd.tensor_copy(wq_hi[:, :], wq_f[:, :])
            nc.gpsimd.tensor_copy(wd_hi[:, :], wd_f[:, :]).then_inc(proj_hi_set, 1)
            pool.wait_ge(proj_hi_set, 1)
            nc.gpsimd.tensor_tensor(wq_lo[:, :], wq_f[:, :], wq_hi[:, :].bitcast(fp32), ALU.subtract)
            nc.gpsimd.tensor_tensor(wd_lo[:, :], wd_f[:, :], wd_hi[:, :].bitcast(fp32),
                                    ALU.subtract).then_inc(proj_split, 1)
            pool.wait_ge(proj_split, 1)
            nc.gpsimd.memset(kst[0][3 * HD:3 * HD + 1, :, :].bitcast(fp32), 1.0).then_inc(stack_ones, 1)
            pool.sem_inc(yg_added, 2)
            pool.wait_ge(stack_ones, 1)
            pool.wait_ge(res_in, 16)

            def add_gated(m, k):
                pool.wait_ge(yg_done, 2 + m)
                pool.wait_ge(yg_added, 2 + m)
                cols = slice(W * (k % CH), W * (k % CH + 1))
                nc.gpsimd.tensor_tensor(acc[:, cols], acc[:, cols], yg[:, k % 2, :], ALU.add).then_inc(yg_added, 1)

            for k in range(ITEMS):
                add_gated(k, k)
                if k < CH:
                    cols = slice(W * k, W * (k + 1))
                    if k == 0:
                        pool.wait_ge(xlo_set, CH)
                        pool.wait_ge(gid_in, 16)
                    else:
                        pool.wait_ge(same_a, 3 * k)
                    nc.gpsimd.tensor_tensor(same[:, :], xhi[:, cols].bitcast(fp32), xlo[:, cols].bitcast(fp32),
                                            ALU.add).then_inc(same_a, 1)
                    pool.wait_ge(same_a, 3 * k + 1)
                    nc.gpsimd.tensor_tensor(same[:, :], same[:, :], gid[:, cols], ALU.mult).then_inc(same_a, 1)
                    pool.wait_ge(same_a, 3 * k + 2)
                    pool.wait_ge(yg_added, 3 + k)
                    nc.gpsimd.tensor_tensor(acc[:, cols], acc[:, cols], same[:, :], ALU.add).then_inc(same_a, 1)
                elif k == CH:
                    pool.wait_ge(same_a, 3 * CH)
            with pool.Fori(1, PAIRS) as p:
                for k in range(ITEMS):
                    add_gated(ITEMS * p + k, k)

            def accumulate(i, c, first):
                pool.wait_ge(exp_done, ST * i + G * (c + 1))
                total = Psum[c // 4]
                if c % 4 == 1:
                    if not first:
                        pool.wait_ge(den_done, 2 * i - 1 + c // 4)
                    other = P[(c - 1) % 4]
                else:
                    pool.wait_ge(psum_done, SUMS * i + absorbed(c) - 1)
                    other = total
                nc.gpsimd.tensor_tensor(total[:, :, :], other[:, :, :], P[c % 4][:, :, :],
                                        ALU.add).then_inc(psum_done, 1)

            def batch(b, first, last):
                for k in range(3 if last else 4):
                    for c in (1, 2, 3, 5, 6, 7):
                        accumulate(4 * b + k, c, first and k == 0)

            sections(pool, batch)

        @block.scalar
        def _(act):
            act.sem_inc(gelu_done, 4)

            def deviations(r):
                act.wait_ge(var_set, r + 1)
                tiles = slice(8 * r, 8 * r + 8)
                nc.scalar.activation(rstd[:, tiles], rstd[:, tiles], ACT.Sqrt).then_inc(std_set, 1)

            def norm(c):
                act.wait_ge(recip_set, c // 2 + 1)
                for t in range(4 * c, 4 * c + 2):
                    last = nc.scalar.activation(x[:, t, :], x[:, t, :], ACT.Identity, bias=shift[:, t:t + 1],
                                                scale=rstd[:, t:t + 1])
                last.then_inc(xn_act, 1)

            deviations(0)
            norm(0)
            norm(1)
            for c in range(CH):
                if c % 2 == 0 and c // 2 + 1 < 4:
                    deviations(c // 2 + 1)
                cols = slice(W * c, W * (c + 1))
                act.wait_ge(x_turned, c + 1)
                nc.scalar.copy(xhi[:, cols], aux[c % AB][:, :])
                if c >= 2:
                    act.wait_ge(logits_set, c - 1)
                nc.scalar.copy(xTf[:, c % 2, :], aux[c % AB][:, :]).then_inc(xT_copied, 1)
                if c + 2 < CH:
                    norm(c + 2)
            act.wait_ge(shifted, 1)
            nc.scalar.activation(prob[:, :, :], prob[:, :, :], ACT.Exp).then_inc(exped, 1)

            def gelu(p, k, beside):
                m = ITEMS * p + k
                for c in range(FC):
                    u = FC * m + c
                    act.wait_ge(up_done, u + 1)
                    if c == 0:
                        act.wait_ge(down_done, m + 1)
                    act.wait_ge(hlo_done, u + 1)
                    src = up_ps[c][:, :]
                    nc.scalar.activation(h_hi[:, k % 2, c, :], src, ACT.Gelu)
                    nc.scalar.activation(hf[:, c % 2, :], src, ACT.Gelu).then_inc(gelu_done, 1)
                    for no, (kind, j) in beside[c]:
                        project(0, 0, kind, j, no)
                for us in beside[FC:]:
                    for no, (kind, j) in us:
                        project(0, 0, kind, j, no)

            with act.Fori(0, PAIRS - 1) as p:
                for k in range(ITEMS):
                    gelu(p, k, [[]] * 2 * FC)

            def exps(b, first, last):
                for g, k, c, units in numbered(first, last):
                    i, start = 4 * b + k, first and k == 0
                    for h, us in enumerate(places(units)):
                        for kind, j, no in us:
                            project(b, g + 1, kind, j, no)
                        if h == G and c == 0 and not start:
                            copy_o(i - 1, first and k == 1)
                        if h >= G:
                            continue
                        if start and c == 2 and h == 0:
                            act.wait_ge(yg_added, 2 + CH * E)
                        u = ST * k + G * c + h
                        act.wait_ge(st_ready, 4 * ST * b + u + 1)
                        if h == 0 and not (start and c < 4):
                            act.wait_ge(pv_done, 8 * i + c - 3)
                            if last and k == 3 and c >= 4:
                                act.wait_ge(last_psum, absorbed(c - 4))
                            else:
                                act.wait_ge(psum_done, SUMS * i + absorbed(c - 4) if c >= 4
                                            else SUMS * (i - 1) + absorbed(c + 4))
                        nc.scalar.activation(P[c % 4][:, h, :], st[u % 3][:, :], ACT.Exp,
                                             scale=SCALE).then_inc(exp_done, 1)

            def copy_o(i, start):
                act.wait_ge(pv_done, 8 * i + 8)
                if not start:
                    act.wait_ge(on_done, i)
                nc.scalar.copy(oT[:, :], ps_o[:, :]).then_inc(o_copied, 1)

            def project(b, g, kind, j, no):
                cols, par, bank = slice(W * j, W * (j + 1)), g % 2, no % AB
                if kind not in ("q", "k", "latent", "v"):
                    return
                act.wait_ge(aux_ready, AUX_BATCH * b + no + 1)
                if kind in ("q", "k"):
                    if j == 0 and g:
                        act.wait_ge(stacked[1 - par], STACK * (b + 1))
                    dst = q_hi if kind == "q" else k_hi
                    nc.scalar.copy(dst[:, cols], aux[bank][:, :]).then_inc(hi_done, 1)
                elif kind == "latent":
                    nc.scalar.copy(lat[:, cols], aux[bank][0:R, :]).then_inc(aux_free[bank], 1)
                else:
                    nc.scalar.copy(v[par][:, 4 * j:4 * j + 4, :],
                                   aux[bank][:, :].rearrange("p (t d) -> p t d", t=4)).then_inc(aux_free[bank], 1)

            for k in range(ITEMS):
                gelu(PAIRS - 1, k, beside_item(k, True))
            nc.scalar.activation(warm[:, :], ones[:, 0:1], ACT.Exp)
            act.wait_ge(down_done, 2 + CH * E)
            sections(act, exps)
            act.wait_ge(pv_done, 8 * 4 * B)
            act.wait_ge(on_done, 4 * B - 1)
            nc.scalar.copy(oT[:, :], ps_o[:, :]).then_inc(o_copied, 1)

        @block.vector
        def _(dve):
            links = [0]

            def link(ins):
                links[0] += 1
                ins.then_inc(chain, 1)
                dve.wait_ge(chain, links[0])

            dve.sem_inc(hlo_done, 2)
            dve.sem_inc(yg_done, 1)

            def split_weights(e, par):
                dve.wait_ge(w_in, 32 * e + 32)
                nc.vector.tensor_copy(w1_hi[:, par, :], w1_f[:, :])
                nc.vector.tensor_copy(w2_hi[:, par, :, :], w2_f[:, :, :]).then_inc(w_hi_set, 1)
                dve.wait_ge(w_hi_set, e + 1)
                nc.vector.tensor_tensor(w1_lo[:, par, :], w1_f[:, :], w1_hi[:, par, :].bitcast(fp32), ALU.subtract)
                nc.vector.tensor_tensor(w2_lo[:, par, :, :], w2_f[:, :, :], w2_hi[:, par, :, :].bitcast(fp32),
                                        ALU.subtract).then_inc(w_split, 1)

            def moments(r):
                tiles = range(8 * r, 8 * r + 8)
                dve.wait_ge(x_in[r], 16)
                for t in tiles:
                    last = nc.vector.bn_stats(stats[:, t, :], x[:, t, :])
                link(last)
                for t in tiles:
                    last = nc.vector.bn_aggr(mv[:, t, :], stats[:, t, :])
                link(last)
                nc.vector.tensor_scalar(rstd[:, 8 * r:8 * r + 8], mv[:, 8 * r:8 * r + 8, 1], EPS, None,
                                        ALU.add).then_inc(var_set, 1)

            def invert_deviations(r):
                dve.wait_ge(std_set, r + 1)
                tiles = slice(8 * r, 8 * r + 8)
                link(nc.vector.reciprocal(rstd[:, tiles], rstd[:, tiles]))
                nc.vector.scalar_tensor_tensor(out=shift[:, tiles], in0=mv[:, tiles, 0], scalar=-1.0,
                                               in1=rstd[:, tiles], op0=ALU.mult, op1=ALU.mult).then_inc(recip_set, 1)

            def low_part(c):
                dve.wait_ge(xT_copied, c + 1)
                cols = slice(W * c, W * (c + 1))
                nc.vector.tensor_tensor(xlo[:, cols], aux[c % AB][:, :], xhi[:, cols].bitcast(fp32),
                                        ALU.subtract).then_inc(xlo_set, 1)

            def norm(c):
                for t in range(4 * c + 2, 4 * c + 4):
                    last = nc.vector.tensor_scalar(x[:, t, :], x[:, t, :], mv[:, t, 0:1], rstd[:, t:t + 1],
                                                   ALU.subtract, ALU.mult)
                last.then_inc(xn_dve, 1)

            moments(0)
            for r in range(4):
                if r + 1 < 4:
                    moments(r + 1)
                invert_deviations(r)
                norm(2 * r)
                norm(2 * r + 1)
                if r:
                    low_part(2 * r - 2)
                    low_part(2 * r - 1)
            low_part(CH - 2)
            low_part(CH - 1)
            dve.wait_ge(logits_set, CH)
            for half, bank in enumerate((ps_o, ps_d)):
                last = nc.vector.transpose(logitsT[:, half, :, :].rearrange("p t e -> p (t e)"), bank[:, :])
            last.then_inc(logits_read, 1)
            dve.wait_ge(logits_read, 1)
            dve.wait_ge(const_in, CONSTS)
            link(nc.vector.tensor_tensor(prob[:, :, :],
                                         logitsT[:, :, :, :].rearrange("p a t e -> p (a t) e")[:, :, 0:E1],
                                         rb[:, :].unsqueeze(1).to_broadcast([128, TILES, E1]), ALU.add))

            wide = [128, TILES, E1]
            bc = top[:, :].unsqueeze(2).to_broadcast(wide)
            link(nc.vector.reduce_max(top[:, :], prob[:, :, :], AX.X))
            nc.vector.tensor_tensor(prob[:, :, :], prob[:, :, :], bc, ALU.subtract).then_inc(shifted, 1)
            dve.wait_ge(exped, 1)
            link(nc.vector.reduce_sum(top[:, :], prob[:, :, :], AX.X))
            link(nc.vector.reciprocal(top[:, :], top[:, :]))
            link(nc.vector.tensor_tensor(prob[:, :, :], prob[:, :, :], bc, ALU.mult))
            dve.wait_ge(zeroed, 4)

            def choose(src, onehot):
                link(nc.vector.reduce_max(top[:, :], src, AX.X))
                link(nc.vector.tensor_tensor(key[:, :, :], src, bc, ALU.is_equal))
                link(nc.vector.tensor_tensor(key[:, :, :], key[:, :, :], rank[:, :, :], ALU.mult))
                link(nc.vector.reduce_max(top[:, :], key[:, :, :], AX.X))
                link(nc.vector.tensor_tensor(onehot, key[:, :, :], bc, ALU.is_equal))

            choose(prob[:, :, :], pick[:, :, :])
            link(nc.vector.scalar_tensor_tensor(out=left[:, :, :], in0=pick[:, :, :], scalar=-2.0,
                                                in1=prob[:, :, :], op0=ALU.mult, op1=ALU.add))
            choose(left[:, :, :], key[:, :, :])
            link(nc.vector.tensor_tensor(key[:, :, :], key[:, :, :], pick[:, :, :], ALU.add))
            nc.vector.tensor_tensor(gates[:, :, :].rearrange("p e t -> p t e"), prob[:, :, :], key[:, :, :],
                                    ALU.mult).then_inc(gates_set, 1)
            dve.wait_ge(gates_set, 1)
            nc.vector.transpose(gatesT[:, :, :].rearrange("p e t -> p (e t)"),
                                gates[:, :, :].rearrange("p e t -> p (e t)")).then_inc(gatesT_set, 1)

            def gate(p, k):
                m, par, i = ITEMS * p + k, k // CH, k % CH
                dve.wait_ge(down_done, 3 + m)
                dve.wait_ge(yg_added, 1 + m)
                half, at = i // (CH // 2), W * (i % (CH // 2))
                if at == 0:
                    dve.wait_ge(gbc_in[half], 16 * (2 * p + par) + 16)
                nc.vector.tensor_tensor(yg[:, k % 2, :], ps_o[:, :], gbc[:, half, at:at + W],
                                        ALU.mult).then_inc(yg_done, 1)

            def low(p, k, beside):
                for c in range(FC):
                    dve.wait_ge(gelu_done, 4 + FC * (ITEMS * p + k) + c + 1)
                    nc.vector.tensor_tensor(h_lo[:, k % 2, c, :], hf[:, c % 2, :],
                                            h_hi[:, k % 2, c, :].bitcast(fp32), ALU.subtract).then_inc(hlo_done, 1)
                    for no, (kind, j) in beside[c]:
                        unit(0, 0, 0, kind, j, no)

            def pair(p, last):
                for k in range(1, ITEMS):
                    beside = beside_item(k, last)
                    low(p, k, beside)
                    for us in beside[FC:]:
                        for no, (kind, j) in us:
                            unit(0, 0, 0, kind, j, no)
                    gate(p, k - 1)
                    if k % CH == 2 and not (last and k > CH):
                        split_weights(2 * p + k // CH + 1, (k // CH + 1) % 2)
                if not last:
                    low(p + 1, 0, [[]] * FC)
                gate(p, ITEMS - 1)

            def unit(b, g, k, kind, j, no):
                if kind == "early":
                    kind, k = "max", k + 1
                bank = no % AB
                if kind in ("max", "turn", "out"):
                    dve.wait_ge(aux_ready, AUX_BATCH * b + no + 1)
                if kind == "max":
                    nc.vector.reduce_max(halfmax[:, k % 2, j // 2, j % 2:j % 2 + 1], aux[bank][:, :],
                                         AX.X).then_inc(aux_free[bank], 1)
                    if j == 2 * 4 * G - 1:
                        wait_unit_read(dve, b, no - 1)
                        wait_unit_read(dve, b, no)
                        nc.vector.tensor_tensor(qmax[:, k % 2, :], halfmax[:, k % 2, :, 0], halfmax[:, k % 2, :, 1],
                                                ALU.max).then_inc(qmax_done, 1)
                elif kind == "turn":
                    if not (isinstance(b, int) and b == 0 and k < 2):
                        dve.wait_ge(max_in[k % 2], 16 * (2 * b + k // 2))
                    nc.vector.tensor_scalar(maxT[:, k % 2, :], aux[bank][0:G * 4, 0:128], -1.0, None,
                                            ALU.mult).then_inc(aux_free[bank], 1)
                elif kind in ("q", "k"):
                    hi, lo = (q_hi, q_lo) if kind == "q" else (k_hi, k_lo)
                    dve.wait_ge(hi_done, 4 * (2 * b + g) + j + (1 if kind == "q" else 3))
                    cols = slice(W * j, W * (j + 1))
                    nc.vector.tensor_tensor(lo[:, cols], aux[bank][:, :], hi[:, cols].bitcast(fp32),
                                            ALU.subtract).then_inc(aux_free[bank], 1)
                elif kind == "out":
                    add(b, k - 2, bank)

            def invert(i, last=0):
                dve.wait_ge(den_done, 2 * i + 2 + last)
                nc.vector.transpose(denT[:, :], ps_d[:, :]).then_inc(den_read, 1)
                dve.wait_ge(den_read, i + 1)
                nc.vector.reciprocal(rsmall[:, :],
                                     denT.rearrange("p (a b) -> p a b", b=32)[:, :, 0]).then_inc(rec_done, 1)

            def spread(i):
                dve.wait_ge(rec_done, i + 1)
                nc.vector.transpose(rden[:, :].rearrange("p (a b) -> p a b", b=32),
                                    rsmall[:, :].unsqueeze(2).to_broadcast([128, W // 32, 32])).then_inc(rden_set, 1)

            def normalise(i):
                dve.wait_ge(rden_set, i + 1)
                dve.wait_ge(o_copied, i + 1)
                nc.vector.tensor_tensor(on[:, :], oT[:, :], rden[:, :], ALU.mult).then_inc(on_done, 1)

            def add(b, k, bank):
                cols = bass.ds(T * b + W * (k % 2), W) if k >= 0 else bass.ds(T * b - W, W)
                nc.vector.tensor_tensor(acc[:, cols], acc[:, cols], aux[bank][:, :],
                                        ALU.add).then_inc(aux_free[bank], 1)

            def last_sum(c):
                i, total = 4 * B - 1, Psum[c // 4]
                dve.wait_ge(exp_done, ST * i + G * (c + 1))
                if c % 4 == 1:
                    dve.wait_ge(den_done, 2 * i - 1 + c // 4)
                    other = P[(c - 1) % 4]
                else:
                    dve.wait_ge(last_psum, absorbed(c) - 1)
                    other = total
                nc.vector.tensor_tensor(total[:, :, :], other[:, :, :], P[c % 4][:, :, :],
                                        ALU.add).then_inc(last_psum, 1)

            def batch(b, first, last):
                for g, k, c, units in numbered(first, last):
                    i, start = 4 * b + k, first and k == 0
                    if last and k == 3 and c in (2, 3, 4, 6, 7):
                        last_sum(c - 1)
                    for q, us in enumerate(places(units)):
                        for kind, j, no in us:
                            unit(b, g + 1, k + 1, kind, j, no)
                        if q == 1 and 3 <= c < 6 and not start:
                            (invert, spread, normalise)[c - 3](i - 1)

            low(0, 0, [[]] * FC)
            with dve.Fori(0, PAIRS - 1) as p:
                pair(p, False)
            pair(PAIRS - 1, True)
            sections(dve, batch)
            i = 4 * B - 1
            invert(i, last=1)
            spread(i)
            normalise(i)
            unit(B - 1, 2, 5, "out", 0, LAST_OUT)

        @block.tensor
        def _(pe):
            pe.sem_inc(down_done, 2)
            pe.wait_ge(ident_set, 1)

            def router(c):
                pe.wait_ge(xT_copied, c + 1)
                rows = slice(32 * (c // 2), 32 * (c // 2) + 32)
                nc.tensor.matmul((ps_o, ps_d)[c % 2][rows, :], rw[:, :], xTf[:, c % 2, :], start=True, stop=True,
                                 skip_group_check=True).then_inc(logits_set, 1)

            for c in range(CH):
                pe.wait_ge(xn_act, c + 1)
                pe.wait_ge(xn_dve, c + 1)
                if c >= AB:
                    pe.wait_ge(xlo_set, c - AB + 1)
                for q in range(4):
                    last = nc.tensor.transpose(aux[c % AB][:, 128 * q:128 * q + 128], x[:, 4 * c + q, :], ident[:, :])
                last.then_inc(x_turned, 1)
                if c >= 1:
                    if c == 1:
                        pe.wait_ge(const_in, CONSTS)
                    router(c - 1)
            router(CH - 1)
            pe.wait_ge(xlo_set, CH)

            def up(p, k, beside):
                m, i, par = ITEMS * p + k, k % CH, k // CH
                if i == 0:
                    pe.wait_ge(w_split, 2 * p + par + 1)
                cols = slice(W * i, W * (i + 1))
                for c in range(FC):
                    if c == FC - 1 and k == 0:
                        pe.wait_ge(logits_read, 1)
                    pe.wait_ge(gelu_done, FC * m + c + 1)
                    w = slice(128 * c, 128 * c + 128)
                    split3(up_ps[c][:, :], w1_hi[:, par, w], w1_lo[:, par, w], xhi[:, cols], xlo[:, cols],
                           True, True).then_inc(up_done, 1)
                    for no, (kind, j) in beside[c]:
                        unit(0, 0, 0, kind, j, no)

            def down(p, k, beside):
                m, par = ITEMS * p + k, k // CH
                pe.wait_ge(yg_done, m + 1)
                for c in range(FC):
                    pe.wait_ge(hlo_done, 2 + FC * m + c + 1)
                    last = split3(ps_o[:, :], w2_hi[:, par, c, :], w2_lo[:, par, c, :], h_hi[:, k % 2, c, :],
                                  h_lo[:, k % 2, c, :], c == 0, c == FC - 1)
                    if c == FC - 1:
                        last.then_inc(down_done, 1)
                    for no, (kind, j) in beside[c]:
                        unit(0, 0, 0, kind, j, no)

            def unit(b, g, k, kind, j, no):
                if kind == "early":
                    kind, k = "max", k + 1
                out, par, b_of = aux[no % AB], g % 2, b + g // 2
                if not (g == 0 and no < AB):
                    wait_unit_read(pe, b, no - AB)
                cols = slice(W * j, W * (j + 1))
                if kind == "max":
                    hh, qt, kh = j // 8, (j // 2) % 4, j % 2
                    gp, half = (k // 2) % 2, k % 2
                    if j == 0:
                        pe.wait_ge(stacked[gp], STACK * (b + k // 4 + 1))
                        if k == 0:
                            pe.wait_ge(stack_ones, 1)
                        elif k == 2 and isinstance(b, int) and b == 0:
                            pe.wait_ge(ones_in, 16)
                    q0 = 128 * qt
                    nc.tensor.matmul(out[:, :], qst[gp][0:3 * HD, half, hh, q0:q0 + 128],
                                     kst[gp][0:3 * HD, hh, W * kh:W * kh + W], start=True,
                                     stop=True).then_inc(aux_ready, 1)
                elif kind == "turn":
                    pe.wait_ge(qmax_done, 4 * b + k + 1)
                    nc.tensor.transpose(out[0:G * 4, 0:128], qmax[:, k % 2, :], ident[:, :]).then_inc(aux_ready, 1)
                elif kind == "out":
                    pe.wait_ge(on_done, 4 * b + k - 1)
                    nc.tensor.matmul(out[:, :], wo[:, ((k - 2) % 4) // 2, :], on[:, :], start=True,
                                     stop=True).then_inc(aux_ready, 1)
                elif kind == "latent":
                    toks = bass.ds(T * b_of + W * j, W)
                    split3(out[0:R, :], wd_hi[:, :], wd_lo[:, :], xhi[:, toks], xlo[:, toks], True,
                           True).then_inc(aux_ready, 1)
                elif kind == "q":
                    toks = bass.ds(T * b_of + W * j, W)
                    w = slice(128 * par, 128 * par + 128)
                    split3(out[:, :], wq_hi[:, w], wq_lo[:, w], xhi[:, toks], xlo[:, toks], True,
                           True).then_inc(aux_ready, 1)
                elif kind == "k":
                    nc.tensor.matmul(out[:, :], wk[:, 128 * par:128 * par + 128], lat[:, cols], start=True,
                                     stop=True).then_inc(aux_ready, 1)
                else:
                    for q in range(4):
                        t = 4 * j + q
                        last = nc.tensor.matmul(out[:, 128 * q:128 * q + 128], lat[:, 128 * t:128 * t + 128],
                                                wv[:, 128 * par:128 * par + 128], start=True, stop=True)
                    last.then_inc(aux_ready, 1)

            def scores(b, k, c, h, first):
                gp, half, u = k // 2, k % 2, ST * k + G * c + h
                if not (first and u < 3):
                    pe.wait_ge(exp_done, 4 * ST * b + {0: -2, 1: -1, 2: -3}.get(u, u - 3) + 1)
                if c == 0 and h == 0:
                    pe.wait_ge(max_in[k % 2], 16 * (2 * b + k // 2 + 1))
                nc.tensor.matmul(st[u % 3][:, :], kst[gp][:, h, 128 * c:128 * c + 128], qst[gp][:, half, h, :],
                                 start=True, stop=True).then_inc(st_ready, 1)

            def values(i, k, c, start):
                pe.wait_ge(exp_done, ST * i + G * c + G)
                gp = k // 2
                if c == 0:
                    if start:
                        pe.wait_ge(yg_done, 1 + E * CH)
                    else:
                        pe.wait_ge(o_copied, i)
                for h in range(G):
                    rows = slice(HD * h, HD * (h + 1))
                    last = nc.tensor.matmul(ps_o[rows, :], v[gp][:, c, rows], P[c % 4][:, h, :], start=(c == 0),
                                            stop=(c == KC - 1), skip_group_check=True)
                last.then_inc(pv_done, 1)

            def denominators(i, j, start, last=False):
                if last:
                    pe.wait_ge(last_psum, (3, 5)[j])
                else:
                    pe.wait_ge(psum_done, SUMS * i + absorbed(4 * j + 3))
                if j == 0 and not start:
                    pe.wait_ge(den_read, i)
                for h in range(G):
                    rows = slice(HD * h, HD * (h + 1))
                    end = nc.tensor.matmul(ps_d[rows, :], ones[:, :], Psum[j][:, h, :], start=(j == 0),
                                           stop=(j == 1 and not last), skip_group_check=True)
                end.then_inc(den_done, 1)

            def lagging(i, k, c, first):
                k1 = (k - 1) % 4
                if c == 0:
                    if not first:
                        values(i - 1, k1, KC - 1, False)
                else:
                    values(i, k, c - 1, first)

            def sums(i, k, c, first, last):
                if c == 6:
                    denominators(i, 0, first, last=last and k == 3)
                if c == 2 and not first:
                    denominators(i - 1, 1, False)

            def batch(b, first, last):
                for g, k, c, units in numbered(first, last):
                    i, start = 4 * b + k, first and k == 0
                    for place, us in enumerate(places(units)):
                        for kind, j, no in us:
                            unit(b, g + 1, k + 1, kind, j, no)
                        if place < G:
                            scores(b, k, c, place, first)
                        elif place == G:
                            lagging(i, k, c, start)
                        else:
                            sums(i, k, c, start, last)

            def pair(p, last):
                for k in range(1, ITEMS):
                    beside = beside_item(k, last)
                    up(p, k, beside[:FC])
                    down(p, k - 1, beside[FC:])
                if not last:
                    up(p + 1, 0, [[]] * FC)
                down(p, ITEMS - 1, [[]] * FC)

            up(0, 0, [[]] * FC)
            with pe.Fori(0, PAIRS - 1) as p:
                pair(p, False)
            pe.wait_ge(proj_split, 1)
            pair(PAIRS - 1, True)
            sections(pe, batch)
            i = 4 * B - 1
            denominators(i, 1, False, last=True)
            pe.wait_ge(exp_done, ST * (i + 1))
            for h in range(G):
                rows = slice(HD * h, HD * (h + 1))
                end = nc.tensor.matmul(ps_d[rows, :], ones[:, :], P[(KC - 1) % 4][:, h, :], start=False, stop=True,
                                       skip_group_check=True)
            end.then_inc(den_done, 1)
            values(i, 3, KC - 1, False)
            unit(B - 1, 2, 5, "out", 0, LAST_OUT)


def kernel(L0_attn_x, L0_attn_Wq, L0_attn_Wkv_down, L0_attn_Wk_up, L0_attn_Wv_up, L0_attn_Wo, L0_ffn_router_w,
           L0_ffn_router_b, L0_ffn_w1, L0_ffn_w2):
    import numpy as np
    import concourse.bacc as bacc
    from concourse.bass_utils import run_bass_kernel_spmd

    x = np.ascontiguousarray(L0_attn_x).reshape(N, D)
    arrays = {
        "x_dram": x,
        "xT_dram": np.ascontiguousarray(x.T),
        "wqT_dram": np.ascontiguousarray(np.asarray(L0_attn_Wq).T),
        "wdT_dram": np.ascontiguousarray(np.asarray(L0_attn_Wkv_down).T),
        "wkT_dram": np.ascontiguousarray(np.asarray(L0_attn_Wk_up).T),
        "wvT_dram": np.ascontiguousarray(np.asarray(L0_attn_Wv_up).T),
        "woT_dram": np.ascontiguousarray(np.asarray(L0_attn_Wo).T),
        "rw_dram": np.ascontiguousarray(L0_ffn_router_w),
        "rb_dram": np.ascontiguousarray(L0_ffn_router_b),
        "w1_dram": np.ascontiguousarray(L0_ffn_w1),
        "w2_dram": np.ascontiguousarray(L0_ffn_w2),
    }
    nc = bacc.Bacc("TRN2", target_bir_lowering=False, num_devices=1)
    ins = [nc.dram_tensor(k, a.shape, mybir.dt.from_np(a.dtype), kind="ExternalInput").ap()
           for k, a in arrays.items()]
    out = nc.dram_tensor("outT", (D, N), fp32, kind="ExternalOutput").ap()
    build(nc, *ins, out)
    r = run_bass_kernel_spmd(nc, [arrays], core_ids=[0])
    return np.ascontiguousarray(np.asarray(r.results[0]["outT"]).T).reshape(B, T, D)
```
